# Optimizing a Trainium2 kernel written in Bass

```python
import numpy as np
import jax
import jax.numpy as jnp

def _softmax(x, axis=-1):
    return jax.nn.softmax(x, axis=axis)

def _gelu(x):
    return jax.nn.gelu(x, approximate=True)

def _silu(x):
    return jax.nn.silu(x)

def _sigmoid(x):
    return jax.nn.sigmoid(x)

def _layernorm(x, axis=-1, eps=1e-05):
    m = jnp.mean(x, axis=axis, keepdims=True)
    v = jnp.var(x, axis=axis, keepdims=True)
    return (x - m) / jnp.sqrt(v + eps)

def _scatter_add(tgt, idx, src, axis=0):
    return tgt.at[idx].add(src)

def _segment_sum(src, seg, n):
    return jax.ops.segment_sum(src, seg, n)
kernel_name = 'mk_pixart_resid_d2_seqx_r8_2afe81'

def setup_inputs(seed: int=0):
    np.random.seed(seed)
    _w = jnp.asarray

    def _rec_inputs():
        import jax
        import jax.numpy as jnp
        _rk = jax.random.key(seed)
        x = -0.0002928 + 1 * jax.random.normal(jax.random.fold_in(_rk, 1), (2, 512, 128), jnp.float32)
        _lenS = 512 - jax.random.randint(jax.random.fold_in(_rk, 7), (2,), 0, max(1, 512 // 4) + 1, jnp.int32)
        _lenS2 = 77 - jax.random.randint(jax.random.fold_in(_rk, 8), (2,), 0, max(1, 77 // 4) + 1, jnp.int32)
        _ctx_1024P = jax.random.normal(jax.random.fold_in(_rk, 11), (2, 16, 128), jnp.float32)
        _ctx_1024c = jax.random.dirichlet(jax.random.fold_in(_rk, 511), 0.3 * jnp.ones((16,), jnp.float32), (2, 77))
        _ctx_1024t = jnp.einsum('bsk,bkd->bsd', _ctx_1024c, _ctx_1024P)
        _ctx_1024t = _ctx_1024t * jax.lax.rsqrt(jnp.mean(jnp.square(_ctx_1024t)) + 1e-12) * 0.953939
        ctx_1024 = -1.39393e-06 + 0.999914 * (_ctx_1024t + 0.3 * jax.random.normal(jax.random.fold_in(_rk, 611), (2, 77, 128), jnp.float32))
        condB_tau = jax.random.uniform(jax.random.fold_in(_rk, 12), (2,), jnp.float32, 0.0, 1.23395)
        fside_BxS2_0 = -0.00205293 + 0.99739 * jax.random.normal(jax.random.fold_in(_rk, 13), (2, 77), jnp.float32)
        return (x, ctx_1024, condB_tau, fside_BxS2_0)
    x, ctx_1024, condB_tau, fside_BxS2_0 = _rec_inputs()

    def _L0_xcond_setup():
        import jax, jax.numpy as jnp
        import numpy as np
        B, S, D, H = (2, 256, 128, 16)
        DK = D // H

        def _split_heads(x):
            b, s, _ = x.shape
            return x.reshape(b, s, H, DK).transpose(0, 2, 1, 3)
        key = jax.random.key(seed)
        ks = jax.random.split(key, 14)
        inp = {'query': jax.random.normal(ks[0], (B, S, D), jnp.float32), 'key': jax.random.normal(ks[1], (B, S, D), jnp.float32), 'value': jax.random.normal(ks[2], (B, S, D), jnp.float32), 'tau': jax.random.uniform(ks[3], (B, 1), jnp.float32, 0.5, 1.5), 'delta': jax.random.normal(ks[4], (B, S), jnp.float32)}
        sc = 1.0 / np.sqrt(D)
        for i, name in enumerate(['q', 'k', 'v', 'o']):
            inp[f'W{name}'] = jax.random.normal(ks[5 + 2 * i], (D, D), jnp.float32) * sc
            inp[f'b{name}'] = jax.random.normal(ks[6 + 2 * i], (D,), jnp.float32) * 0.01
        return inp
    _L0_xcond_all = _L0_xcond_setup()
    _L0_xcond_in = {k: v for k, v in _L0_xcond_all.items() if k in ('Wq', 'bq', 'Wk', 'bk', 'Wv', 'bv', 'Wo', 'bo')}
    del _L0_xcond_all

    def _L0_ffn_setup():
        import jax, jax.numpy as jnp
        import numpy as np
        B, S, D, F, E, R = (4, 256, 128, 512, 8, 4)
        key = jax.random.key(seed)
        ks = jax.random.split(key, 8)
        s_in = 1.0 / np.sqrt(D)
        s_ff = 1.0 / np.sqrt(F)
        return {'hidden_states': jax.random.normal(ks[0], (B, S, D), jnp.float32), 'gate_W': jax.random.normal(ks[1], (E, D), jnp.float32) * s_in, 'gate_b': jnp.zeros((E,), jnp.float32), 'wi_W': jax.random.normal(ks[2], (F, D), jnp.float32) * s_in, 'wi_b': jnp.zeros((F,), jnp.float32), 'wo_W': jax.random.normal(ks[3], (D, F), jnp.float32) * s_ff, 'wo_b': jnp.zeros((D,), jnp.float32), 'lora_A': jax.random.normal(ks[4], (E, R, D), jnp.float32) * s_in, 'lora_B': jax.random.normal(ks[5], (E, F, R), jnp.float32) * 0.02}
    _L0_ffn_all = _L0_ffn_setup()
    _L0_ffn_in = {k: v for k, v in _L0_ffn_all.items() if k in ('gate_W', 'gate_b', 'wi_W', 'wi_b', 'wo_W', 'wo_b', 'lora_A', 'lora_B')}
    del _L0_ffn_all

    def _L1_xcond_setup():
        import jax, jax.numpy as jnp
        import numpy as np
        D_MODEL = 128
        N_HEADS = 16
        key = jax.random.key(seed)
        ks = jax.random.split(key, 16)
        B, L, S, D = (4, 256, 256, D_MODEL)
        inp = {'q': jax.random.normal(ks[0], (B, L, D), jnp.float32), 'k': jax.random.normal(ks[1], (B, S, D), jnp.float32), 'v': jax.random.normal(ks[2], (B, S, D), jnp.float32), 'tau': jax.random.uniform(ks[3], (B, 1), jnp.float32, 0.5, 1.5), 'delta': jax.random.normal(ks[4], (B, S), jnp.float32)}
        s = 1.0 / np.sqrt(D)
        inp['Wq'] = jax.random.normal(ks[5], (D, D), jnp.float32) * s
        inp['bq'] = jnp.zeros((D,), jnp.float32)
        inp['Wk'] = jax.random.normal(ks[6], (D, D), jnp.float32) * s
        inp['bk'] = jnp.zeros((D,), jnp.float32)
        inp['Wv'] = jax.random.normal(ks[7], (D, D), jnp.float32) * s
        inp['bv'] = jnp.zeros((D,), jnp.float32)
        inp['Wo'] = jax.random.normal(ks[8], (D, D), jnp.float32) * s
        inp['bo'] = jnp.zeros((D,), jnp.float32)
        return inp
    _L1_xcond_all = _L1_xcond_setup()
    _L1_xcond_in = {k: v for k, v in _L1_xcond_all.items() if k in ('Wq', 'bq', 'Wk', 'bk', 'Wv', 'bv', 'Wo', 'bo')}
    del _L1_xcond_all

    def _L1_ffn_setup():
        import jax, jax.numpy as jnp
        import numpy as np
        B, S, D = (4, 256, 128)
        E, F = (8, 512)
        key = jax.random.key(seed)
        ks = jax.random.split(key, 5)
        x = jax.random.normal(ks[0], (B, S, D), dtype=jnp.float32)
        switch_w = jax.random.normal(ks[1], (D, E), dtype=jnp.float32) * D ** (-0.5)
        switch_b = jnp.zeros((E,), dtype=jnp.float32)
        w1 = jax.random.normal(ks[2], (E, D, F), dtype=jnp.float32) * D ** (-0.5)
        b1 = jnp.zeros((E, F), dtype=jnp.float32)
        w2 = jax.random.normal(ks[3], (E, F, D), dtype=jnp.float32) * F ** (-0.5)
        b2 = jnp.zeros((E, D), dtype=jnp.float32)
        return {'x': x, 'switch_w': switch_w, 'switch_b': switch_b, 'w1': w1, 'b1': b1, 'w2': w2, 'b2': b2}
    _L1_ffn_all = _L1_ffn_setup()
    _L1_ffn_in = {k: v for k, v in _L1_ffn_all.items() if k in ('switch_w', 'switch_b', 'w1', 'b1', 'w2', 'b2')}
    del _L1_ffn_all
    return {'x': x, 'ctx_1024': ctx_1024, 'condB_tau': condB_tau, 'fside_BxS2_0': fside_BxS2_0, 'L0_xcond_Wq': _L0_xcond_in['Wq'], 'L0_xcond_bq': _L0_xcond_in['bq'], 'L0_xcond_Wk': _L0_xcond_in['Wk'], 'L0_xcond_bk': _L0_xcond_in['bk'], 'L0_xcond_Wv': _L0_xcond_in['Wv'], 'L0_xcond_bv': _L0_xcond_in['bv'], 'L0_xcond_Wo': _L0_xcond_in['Wo'], 'L0_xcond_bo': _L0_xcond_in['bo'], 'L0_ffn_gate_W': _L0_ffn_in['gate_W'], 'L0_ffn_gate_b': _L0_ffn_in['gate_b'], 'L0_ffn_wi_W': _L0_ffn_in['wi_W'], 'L0_ffn_wi_b': _L0_ffn_in['wi_b'], 'L0_ffn_wo_W': _L0_ffn_in['wo_W'], 'L0_ffn_wo_b': _L0_ffn_in['wo_b'], 'L0_ffn_lora_A': _L0_ffn_in['lora_A'], 'L0_ffn_lora_B': _L0_ffn_in['lora_B'], 'L1_xcond_Wq': _L1_xcond_in['Wq'], 'L1_xcond_bq': _L1_xcond_in['bq'], 'L1_xcond_Wk': _L1_xcond_in['Wk'], 'L1_xcond_bk': _L1_xcond_in['bk'], 'L1_xcond_Wv': _L1_xcond_in['Wv'], 'L1_xcond_bv': _L1_xcond_in['bv'], 'L1_xcond_Wo': _L1_xcond_in['Wo'], 'L1_xcond_bo': _L1_xcond_in['bo'], 'L1_ffn_switch_w': _L1_ffn_in['switch_w'], 'L1_ffn_switch_b': _L1_ffn_in['switch_b'], 'L1_ffn_w1': _L1_ffn_in['w1'], 'L1_ffn_b1': _L1_ffn_in['b1'], 'L1_ffn_w2': _L1_ffn_in['w2'], 'L1_ffn_b2': _L1_ffn_in['b2']}

def reference(x, ctx_1024, condB_tau, fside_BxS2_0, L0_xcond_Wq, L0_xcond_bq, L0_xcond_Wk, L0_xcond_bk, L0_xcond_Wv, L0_xcond_bv, L0_xcond_Wo, L0_xcond_bo, L0_ffn_gate_W, L0_ffn_gate_b, L0_ffn_wi_W, L0_ffn_wi_b, L0_ffn_wo_W, L0_ffn_wo_b, L0_ffn_lora_A, L0_ffn_lora_B, L1_xcond_Wq, L1_xcond_bq, L1_xcond_Wk, L1_xcond_bk, L1_xcond_Wv, L1_xcond_bv, L1_xcond_Wo, L1_xcond_bo, L1_ffn_switch_w, L1_ffn_switch_b, L1_ffn_w1, L1_ffn_b1, L1_ffn_w2, L1_ffn_b2):
    import jax
    import jax.numpy as jnp

    def _L0_xcond_ref(query, key, value, tau, delta, Wq, bq, Wk, bk, Wv, bv, Wo, bo):
        import jax, jax.numpy as jnp
        import numpy as np
        B, S, D, H = (2, 256, 128, 16)
        DK = D // H

        def _split_heads(x):
            b, s, _ = x.shape
            return x.reshape(b, s, H, DK).transpose(0, 2, 1, 3)
        q = _split_heads(query @ Wq.T + bq)
        k = _split_heads(key @ Wk.T + bk)
        v = _split_heads(value @ Wv.T + bv)
        scores = jnp.einsum('bhqd,bhkd->bhqk', q, k)
        scores = scores * tau[:, :, None, None] + delta[:, None, None, :]
        scores = scores / jnp.sqrt(jnp.asarray(DK, scores.dtype))
        p_attn = jax.nn.softmax(scores, axis=-1)
        x = jnp.einsum('bhqk,bhkd->bhqd', p_attn, v)
        x = x.transpose(0, 2, 1, 3).reshape(query.shape[0], -1, H * DK)
        return x @ Wo.T + bo

    def _L0_ffn_ref(hidden_states, gate_W, gate_b, wi_W, wi_b, wo_W, wo_b, lora_A, lora_B):
        import jax, jax.numpy as jnp
        import numpy as np
        B, S, D, F, E, R = (4, 256, 128, 512, 8, 4)
        x = hidden_states
        logits = jnp.einsum('bsd,ed->bse', x, gate_W) + gate_b
        top1 = jnp.argmax(jax.nn.softmax(logits, axis=-1), axis=-1)
        base = jnp.einsum('bsd,fd->bsf', x, wi_W) + wi_b
        out = jnp.zeros_like(x)
        for i in range(lora_A.shape[0]):
            lora = jnp.einsum('bsr,fr->bsf', jnp.einsum('bsd,rd->bsr', x, lora_A[i]), lora_B[i])
            inter = jax.nn.relu(base + lora)
            expert_out = jnp.einsum('bsf,df->bsd', inter, wo_W) + wo_b
            mask = (top1 == i).astype(x.dtype)[..., None]
            out = out + mask * expert_out
        return out

    def _L1_xcond_ref(q, k, v, tau, delta, Wq, bq, Wk, bk, Wv, bv, Wo, bo):
        import jax, jax.numpy as jnp
        import numpy as np
        D_MODEL = 128
        N_HEADS = 16
        B, L, D = q.shape
        S = k.shape[1]
        H = N_HEADS
        E = D // H
        qh = (q @ Wq.T + bq).reshape(B, L, H, E)
        kh = (k @ Wk.T + bk).reshape(B, S, H, E)
        vh = (v @ Wv.T + bv).reshape(B, S, H, E)
        scale = 1.0 / np.sqrt(E).astype(np.float32)
        scores = jnp.einsum('blhe,bshe->bhls', qh, kh)
        scores = scores * tau[:, None, None, :] + delta[:, None, None, :]
        a = jax.nn.softmax(scale * scores, axis=-1)
        out = jnp.einsum('bhls,bshd->blhd', a, vh).reshape(B, L, D)
        return out @ Wo.T + bo

    def _L1_ffn_ref(x, switch_w, switch_b, w1, b1, w2, b2):
        import jax, jax.numpy as jnp
        import numpy as np
        B, S, D = (4, 256, 128)
        E, F = (8, 512)
        b, s, d = x.shape
        t = x.reshape(-1, d)
        logits = t @ switch_w + switch_b
        route_prob = jax.nn.softmax(logits, axis=-1)
        route_prob_max = jnp.max(route_prob, axis=-1)
        routes = jnp.argmax(route_prob, axis=-1)
        out = jnp.zeros_like(t)
        n_experts = w1.shape[0]
        for e in range(n_experts):
            h = jax.nn.gelu(t @ w1[e] + b1[e])
            y = h @ w2[e] + b2[e]
            mask = (routes == e)[:, None]
            out = jnp.where(mask, y, out)
        out = out * route_prob_max[:, None]
        return out.reshape(b, s, d)
    x = x + _L0_xcond_ref(_layernorm(x, axis=-1), ctx_1024, ctx_1024, condB_tau[:, None], fside_BxS2_0, L0_xcond_Wq, L0_xcond_bq, L0_xcond_Wk, L0_xcond_bk, L0_xcond_Wv, L0_xcond_bv, L0_xcond_Wo, L0_xcond_bo)
    x = x + _L0_ffn_ref(_layernorm(x, axis=-1), L0_ffn_gate_W, L0_ffn_gate_b, L0_ffn_wi_W, L0_ffn_wi_b, L0_ffn_wo_W, L0_ffn_wo_b, L0_ffn_lora_A, L0_ffn_lora_B)
    x = x + _L1_xcond_ref(_layernorm(x, axis=-1), ctx_1024, ctx_1024, condB_tau[:, None], fside_BxS2_0, L1_xcond_Wq, L1_xcond_bq, L1_xcond_Wk, L1_xcond_bk, L1_xcond_Wv, L1_xcond_bv, L1_xcond_Wo, L1_xcond_bo)
    x = x + _L1_ffn_ref(_layernorm(x, axis=-1), L1_ffn_switch_w, L1_ffn_switch_b, L1_ffn_w1, L1_ffn_b1, L1_ffn_w2, L1_ffn_b2)
    return x

_drawn_inputs = setup_inputs


def setup_inputs(seed=0):
    import zlib

    import numpy as np

    out = dict(_drawn_inputs(seed))
    spreads = {'L0_ffn_gate_b': (0.0, 0.8),
     'L0_ffn_wi_b': (0.0, 0.1),
     'L0_ffn_wo_b': (0.0, 0.1),
     'L1_xcond_bq': (0.0, 0.545),
     'L1_xcond_bk': (0.0, 2.0),
     'L1_xcond_bv': (0.0, 0.1),
     'L1_xcond_bo': (0.0, 0.1),
     'L1_ffn_switch_b': (0.0, 0.28),
     'L1_ffn_b1': (0.0, 0.364),
     'L1_ffn_b2': (0.0, 0.1)}
    factors = {'L0_xcond_bq': 29.482, 'L0_xcond_bk': 64.0, 'L0_xcond_bv': 4.025, 'L0_xcond_bo': 3.399}
    for name, (base, spread) in spreads.items():
        noise = np.random.default_rng([zlib.crc32(name.encode()), seed]).standard_normal(out[name].shape)
        drawn = base * np.exp(spread * noise) if base else spread * noise
        out[name] = jnp.asarray(drawn.astype(out[name].dtype))
    for name, factor in factors.items():
        out[name] = (out[name] * factor).astype(out[name].dtype)
    return out
```

```python
from contextlib import ExitStack

import numpy as np
import concourse.bass as bass
from concourse import mybir

F32 = mybir.dt.float32
F32R = mybir.dt.float32r
BF16 = mybir.dt.bfloat16
I32 = mybir.dt.int32
ALU = mybir.AluOpType
ACT = mybir.ActivationFunctionType
AX = mybir.AxisListType

B = 2
S = 512
D = 128
NQ = S // 128
KEYS = 77
H = 16
DK = D // H
G = 4
HG = H // G
GK = HG * KEYS
HALF = 8
NT = 5
STARTS = [0, 123, 246, 370, 493]
WIDTHS = [123, 123, 124, 123, 123]
TW = 124
GP = 370
PAD = GP - GK
QR = 3 * 32
ONES = QR
KR = QR + 2 + HG
VC = DK + 1
VW = 128
E = 8
R = 4
F = 512
NF = F // 128
EPS = 1e-5
TILES = B * NQ
NS = TILES + E - 1
RW = 2 * D + 4
R_P, R_ID = 2 * D, 2 * D + 1
LOADS = [(0, 1), (1, 3), (3, 6), (6, 10), (10, NS)]
NHB = 3
RS8 = 1.0 / float(np.sqrt(np.float32(DK)))

A_K, A_Q, A_V, A_O = 0, G * QR, 2 * G * QR, 2 * G * QR + D
A_BK = A_O + D
A_BQ = A_BK + G
A_BV = A_BQ + G
A_N = A_BV + 1
C_ID = 0
C_VM = C_ID + 128
C_KM = C_VM + NT * HALF
C_EW = C_KM + HG
C_SEL = C_EW + E
C_NEG = C_SEL + 2
C_TAIL = C_NEG + HG
C_SID = C_TAIL + 4 * TILES
C_THR = C_SID + NS
C_LOW = C_THR + TILES
C_T = C_LOW + E * E
C_TRI = C_T + NS
C_N = C_TRI + 128
R_BO0, R_WOB, R_BO1, R_GB, R_SB = 0, D, 2 * D, 3 * D, 3 * D + E
R_N = R_SB + E
W_GA, W_WI, W_WO = 0, E + E * R, E + E * R + F
W_WIB = W_WO + NF * D
W_N = W_WIB + NF


def schedule():
    steps = []

    def attention_front(l, b):
        return [("ln", 2 * l, b), ("xt", 2 * l, b), ("q", l, b)]

    def maxima(l, b):
        return [("max", l, b, i) for i in range(NQ * G)] + [("mt", l, b)]

    def core(l, b):
        out = [("sc", l, b, 0)]
        for t in range(1, 2 * NT):
            out += [("sc", l, b, t), ("pv", l, b, t - 1)]
        return out + [("pv", l, b, 2 * NT - 1), ("on", l, b)]

    def attention_back(l, b):
        return [("ot", l, b), ("wo", l, b)]

    def ffn0(b):
        return [("ln", 1, b), ("xt", 1, b), ("gate", b), ("ut", b)] + [("hid", b, k) for k in range(NF)] + [("out", b)]

    def merge(a, c):
        out, n = [], 0
        for i, s in enumerate(a):
            out.append(s)
            while n * len(a) < (i + 1) * len(c):
                out.append(c[n])
                n += 1
        return out

    kv = lambda l: [("kp", l)] + [("vp", l, b, j) for b in range(B) for j in range(NT)]
    steps += [("ln", 0, 0), ("kp", 0), ("xt", 0, 0), ("q", 0, 0), ("ln", 0, 1), ("xt", 0, 1), ("q", 0, 1)]
    steps += [("km", 0, 0), ("km", 0, 1)]
    steps += kv(0)[1:]
    steps += maxima(0, 0)
    steps += merge(core(0, 0), maxima(0, 1))
    steps += merge(core(0, 1), attention_back(0, 0) + ffn0(0) + kv(1) + attention_front(1, 0))
    steps += [("km", 1, 0), ("km", 1, 1)]
    steps += maxima(1, 0)
    steps += merge(core(1, 0), attention_back(0, 1) + ffn0(1) + attention_front(1, 1) + maxima(1, 1))
    steps += merge(core(1, 1), attention_back(1, 0) + [("ln", 3, 0), ("xt", 3, 0), ("route", 0), ("ct", 0), ("b2", 0)])
    steps += attention_back(1, 1) + [("ln", 3, 1), ("xt", 3, 1), ("route", 1), ("ct", 1), ("b2", 1)]
    return steps + [("rank",)]


def order(steps):
    counts, nth = {}, {}
    for s in steps:
        kind = "x" if s[0] in ("wo", "out") else s[0]
        nth[s] = counts[kind] = counts.get(kind, -1) + 1
        if s[0] == "xt" and s[1] < 3:
            nth["pre", s[1], s[2]] = counts["pre"] = counts.get("pre", -1) + 1
    return nth


def banks(steps):
    uses = {}
    for s in steps:
        kind = s[0]
        keys = []
        if kind == "kp":
            keys = [(*s, 0), (*s, 1)]
        elif kind == "q":
            keys = [(*s, g) for g in range(G)]
        elif kind in ("xt", "vp", "mt", "ot", "wo", "gate", "ut", "hid", "out", "route", "ct", "b2", "rank"):
            keys = [s]
        for k in keys:
            n = len(uses)
            uses[k] = (n % 2, n // 2)
    return uses


def build(nc, x, ctx3, att0, att1, consts, rows, delta, tau, ffn0w, loraB, sw, w1, b1, w2, b2, out):
    steps = schedule()
    use = banks(steps)
    nth = order(steps)
    before = {}
    for i in range(2):
        mine = [k for k in use if use[k][0] == i]
        before.update(zip(mine[1:], mine))
    stages = ExitStack()
    with stages:
        def sb(name, shape, dt=F32):
            return stages.enter_context(nc.sbuf_tensor(name, shape, dt))

        def sem(name):
            return stages.enter_context(nc.semaphore(name))

        X = sb("X", [128, B, NQ, D])
        CTX = sb("CTX", [128, B, 3 * KEYS])
        ATT = [sb(f"ATT{l}", [128, A_N]) for l in range(2)]
        CON = sb("CON", [128, C_N])
        ROWS = sb("ROWS", [128, R_N])
        DEL = sb("DEL", [128, B * KEYS])
        TAU = sb("TAU", [128, B])
        W0 = sb("W0", [128, W_N])
        LB = sb("LB", [128, F])
        SW = sb("SW", [128, E])
        W1 = sb("W1", [128, E * F])
        B1 = sb("B1", [128, E * NF])
        W2 = sb("W2", [128, E * NF * D])
        B2 = sb("B2", [E, D])

        stats = sb("stats", [128, B, NQ, 6])
        mean_var = sb("mean_var", [128, B, NQ, 2])
        logvar = sb("logvar", [128, B, NQ])
        rstd = sb("rstd", [128, B, NQ])
        eps = sb("eps", [128, 1])
        XN = sb("XN", [128, B, NQ, D])
        XNT = sb("XNT", [128, B, S])
        tau8 = sb("tau8", [128, B])
        dscaled = sb("dscaled", [128, B * KEYS])
        dhigh = sb("dhigh", [128, B * KEYS], F32R)
        drow = sb("drow", [128, B * KEYS])
        dlow = sb("dlow", [128, B * KEYS])
        Kf = sb("Kf", [QR, G, B, KEYS])
        Kt = sb("Kt", [QR, G, B, KEYS])
        Ks = sb("Ks", [QR, G, B, KEYS], F32R)
        KG = sb("KG", [KR, B, G, GP], F32R)
        VP = sb("VP", [TW, 2, B, NT, 2, VW])
        QG = sb("QG", [KR, B, G, S], F32R)
        MR = sb("MR", [128, B, NQ, G, 32])
        NP = 3
        P = sb("P", [TW, NP, S])
        rden = sb("rden", [128, B, NQ, H])
        ON = sb("ON", [128, B, NQ, D])
        OT = sb("OT", [128, B, S])
        lg = sb("lg", [128, B, NQ, E])
        lmax = sb("lmax", [128, B, NQ])
        eq = sb("eq", [128, B, NQ, E])
        first = sb("first", [128, B, NQ])
        hot = sb("hot", [128, B, NQ, E])
        U3 = sb("U3", [128, B, NQ, QR])
        U = sb("U", [QR, B, S], F32R)
        LS = sb("LS", [QR, F], F32R)
        HT = sb("HT", [128, B, NF, S])
        ROW = sb("ROW", [128, TILES, RW])
        hotb = sb("hotb", [128, TILES, E], BF16)
        trib = sb("trib", [128, 128], BF16)
        onesb = sb("onesb", [128, 128], BF16)
        above = sb("above", [128, E, TILES])
        tiles_of = sb("tiles_of", [128, E])
        lower = sb("lower", [128, E, E])
        first_tile = sb("first_tile", [128, E])
        end_tile = sb("end_tile", [128, E])
        place = sb("place", [128, TILES, E])
        slot_f = sb("slot_f", [128, TILES])
        slot = sb("slot", [128, TILES], I32)
        past = sb("past", [1, NS, E])
        tile_f = sb("tile_f", [1, NS + 1])
        tile_e = sb("tile_e", [1, NS + 1], I32)
        XS = sb("XS", [128, NS, RW])
        XST = sb("XST", [128, 2, 128])
        W1C = sb("W1C", [128, 2, F])
        HB = sb("HB", [128, 2, F])
        HG1 = sb("HG1", [128, NHB, F])
        token = sb("token", [128, NS], I32)
        slots = nc.dram_tensor("slots", (NS * 128, RW), F32).ap()
        ex = sb("ex", [128, B, NQ, E])
        esum = sb("esum", [128, B, NQ])
        coef = sb("coef", [128, B, NQ, E])
        CT = OT[0:E]

        scores = [stages.enter_context(nc.psum_tensor(f"scores{i}", [128, 512], F32)) for i in range(2)]
        maxps = [stages.enter_context(nc.psum_tensor(f"maxps{i}", [128, 512], F32)) for i in range(2)]
        acc = [stages.enter_context(nc.psum_tensor(f"acc{i}", [128, 512], F32)) for i in range(2)]
        shared = [stages.enter_context(nc.psum_tensor(f"shared{i}", [128, 512], F32)) for i in range(2)]

        in_x = [sem(f"in_x{b}") for b in range(B)]
        in_ctx, in_con, in_small, in_w0, in_lb = sem("in_ctx"), sem("in_con"), sem("in_small"), sem("in_w0"), sem("in_lb")
        in_att = [sem(f"in_att{l}") for l in range(2)]
        in_moe = sem("in_moe")
        in_w1 = [sem(f"in_w1_{e}") for e in range(E)]
        in_w2 = [sem(f"in_w2_{e}") for e in range(E)]
        zeroed = sem("zeroed")
        erows = sem("erows")
        ones_col = sem("ones_col")
        pre_added = sem("pre_added")
        kg_ready = sem("kg_ready")
        full = [sem(f"full{i}") for i in range(2)]
        stats_ready = sem("stats_ready")
        rstd_ready = sem("rstd_ready")
        act_chain = sem("act_chain")
        dve_chain = sem("dve_chain")
        xn_ready = sem("xn_ready")
        xnt_ready = sem("xnt_ready")
        k_biased = sem("k_biased")
        k_split = sem("k_split")
        tau_ready = sem("tau_ready")
        v_ready = sem("v_ready")
        qh_ready = sem("qh_ready")
        ql_ready = sem("ql_ready")
        m_act = sem("m_act")
        m_dve = sem("m_dve")
        max_full = sem("max_full")
        max_read = sem("max_read")
        scores_ready = sem("scores_ready")
        probs_ready = sem("probs_ready")
        probs_used = sem("probs_used")
        on_ready = sem("on_ready")
        ot_ready = sem("ot_ready")
        x_ready = sem("x_ready")
        u3_ready = sem("u3_ready")
        u_ready = sem("u_ready")
        lb_ready = sem("lb_ready")
        hid_act = sem("hid_act")
        hid_dve = sem("hid_dve")
        lg_ready = sem("lg_ready")
        ex_ready = sem("ex_ready")
        coef_ready = sem("coef_ready")
        ct_ready = sem("ct_ready")
        b2_ready = sem("b2_ready")
        preset = sem("preset")
        rows_set = sem("rows_set")
        blank = sem("blank")
        hot_ready = sem("hot_ready")
        binary = sem("binary")
        rank_read = sem("rank_read")
        slot_ready = sem("slot_ready")
        tile_ready = sem("tile_ready")
        rows_sent = sem("rows_sent")
        slots_in = [sem(f"slots_in{i}") for i in range(len(LOADS))]
        xst_full = sem("xst_full")
        xst_ready = sem("xst_ready")
        w1_ready = sem("w1_ready")
        hidden_full = sem("hidden_full")
        biased = sem("biased")
        gelu_ready = sem("gelu_ready")
        y_full = sem("y_full")
        z_ready = sem("z_ready")
        token_ready = sem("token_ready")
        stored = sem("stored")

        ident = CON[:, C_ID:C_ID + 128]
        hidden = [scores[0], scores[1], shared[0]]

        def bank(key):
            return shared[use[key][0]]

        def reader(key):
            kind = key[0]
            if kind == "kp":
                return k_biased, G * key[1] + 2 * (key[2] + 1)
            if kind == "q":
                return ql_ready, G * nth[key[:3]] + key[3] + 1
            if kind == "mt":
                return [(m_act, 2 * (nth[key] + 1)), (m_dve, 2 * (nth[key] + 1))]
            if kind == "gate":
                return u3_ready, 3 * NQ * (nth[key] + 1)
            if kind == "hid":
                return (hid_dve if key[2] % 2 else hid_act), 2 * key[1] + key[2] // 2 + 1
            by = {"xt": xnt_ready, "vp": v_ready, "ot": ot_ready, "route": lg_ready,
                  "ut": u_ready, "ct": ct_ready, "wo": x_ready, "out": x_ready, "b2": b2_ready}
            return by[kind], nth[key] + 1

        def read(eng, key):
            i, n = use[key]
            eng.wait_ge(full[i], n + 1)

        block = stages.enter_context(nc.Block())

        @block.sync
        def _(sp):
            xv = x.rearrange("(b t p) d -> b p t d", b=B, p=128)
            for b in range(B):
                sp.dma_start(X[:, b], xv[b]).then_inc(in_x[b], 16)
            sp.dma_start(ATT[0][:, :], att0).then_inc(in_att[0], 16)
            sp.dma_start(W0[:, :], ffn0w).then_inc(in_w0, 16)
            sp.dma_start(ATT[1][:, :], att1).then_inc(in_att[1], 16)
            for e in range(E):
                sp.dma_start(W1[:, e * F:(e + 1) * F], w1[:, e]).then_inc(in_w1[e], 16)
                sp.dma_start(W2[:, e * NF * D:(e + 1) * NF * D], w2[:, e]).then_inc(in_w2[e], 16)
            sv = slots.rearrange("(t p) w -> p t w", p=128)
            sp.wait_ge(blank, 2)
            sp.dma_start(sv, XS[:, :, :]).then_inc(preset, 16)
            sp.wait_ge(rows_sent, 16 * TILES)
            for i, (t0, t1) in enumerate(LOADS):
                sp.dma_start(XS[:, t0:t1], sv[:, t0:t1]).then_inc(slots_in[i], 16)

        @block.gpsimd
        def _(pool):
            counts = {}

            def finish(ins, signal):
                counts[signal.name] = counts.get(signal.name, 0) + 1
                ins.then_inc(signal, 1)
                pool.wait_ge(signal, counts[signal.name])

            finish(pool.memset(eps[:, :], EPS), zeroed)
            finish(pool.memset(KG[:, :, :, :].bitcast(F32), 0.0), zeroed)
            finish(pool.memset(QG[ONES:ONES + 2, :, :, :].bitcast(F32), 1.0), zeroed)
            finish(pool.memset(MR[:, :, :, :, :], 0.0), zeroed)
            finish(pool.memset(MR[:, :, :, :, 0:2], 1.0), zeroed)
            finish(pool.memset(VP[:, :, :, :, :, HALF * VC:], 0.0), zeroed)
            pool.wait_ge(in_small, 48)
            finish(pool.tensor_scalar(tau8[:, :], TAU[:, :], RS8, None, ALU.mult), tau_ready)
            r = slice(ONES, KR)
            finish(pool.tensor_scalar(dscaled[r, :], DEL[r, :], RS8, None, ALU.mult), erows)
            finish(pool.tensor_copy(dhigh[r, :], dscaled[r, :]), erows)
            finish(pool.tensor_tensor(dlow[r, :], dscaled[r, :], dhigh[r, :].bitcast(F32), ALU.subtract), erows)
            pool.wait_ge(in_con, 16)
            finish(pool.tensor_scalar(drow[r, :], dhigh[r, :].bitcast(F32), CON[r, C_SEL:C_SEL + 1], None, ALU.mult), erows)
            finish(pool.tensor_scalar(dscaled[r, :], dlow[r, :], CON[r, C_SEL + 1:C_SEL + 2], None, ALU.mult), erows)
            finish(pool.tensor_tensor(drow[r, :], drow[r, :], dscaled[r, :], ALU.add), erows)
            for b in range(B):
                for g in range(G):
                    off = PAD * (g % 2)
                    o = KG[r, b, g, off:off + GK].rearrange("p (h k) -> p h k", h=HG)
                    d3 = drow[r, b * KEYS:(b + 1) * KEYS].unsqueeze(1).to_broadcast([KR - ONES, HG, KEYS])
                    n3 = CON[r, C_NEG:C_NEG + HG].unsqueeze(2).to_broadcast([KR - ONES, HG, KEYS])
                    finish(pool.tensor_tensor(o, d3, n3, ALU.add), erows)
            vm = CON[0:TW, C_VM:C_VM + NT * HALF].rearrange("p (j h) -> p j h", j=NT)
            for l in range(2):
                for b in range(B):
                    for half in range(2):
                        o = VP[:, l, b, :, half, 0:HALF * VC].rearrange("p j (h c) -> p j h c", c=VC)[:, :, :, DK]
                        finish(pool.tensor_copy(o, vm), ones_col)
            kmask = CON[0:QR, C_KM:C_KM + HG]

            def moe_constants():
                finish(pool.memset(XS[:, :, :], 0.0), blank)
                finish(pool.tensor_copy(XS[:, :, R_ID], CON[:, C_SID:C_SID + NS]), blank)
                tail = CON[:, C_TAIL:C_TAIL + 4 * TILES].rearrange("p (t c) -> p t c", c=4)
                finish(pool.tensor_copy(ROW[:, :, 2 * D:RW], tail), rows_set)
                finish(pool.tensor_copy(trib[:, :], CON[:, C_TRI:C_TRI + 128]), binary)
                finish(pool.memset(onesb[:, :], 1.0), binary)

            for s in steps:
                if s == ("km", 1, 0):
                    moe_constants()
                if s[0] == "km":
                    _, l, b = s
                    pool.wait_ge(k_split, l + 1)
                    if l == 1:
                        pool.wait_ge(scores_ready, 2 * NT * (b + 1))
                    for g in range(G):
                        off = PAD * (g % 2)
                        o = KG[0:QR, b, g, off:off + GK].rearrange("p (h k) -> p h k", h=HG)
                        k3 = Ks[:, g, b].bitcast(F32).unsqueeze(1).to_broadcast([QR, HG, KEYS])
                        m3 = kmask.unsqueeze(2).to_broadcast([QR, HG, KEYS])
                        finish(pool.tensor_tensor(o, k3, m3, ALU.mult), kg_ready)
                elif s[0] == "xt" and s[1] < 3:
                    _, st, b = s
                    c = (R_BO0, R_WOB, R_BO1)[st]
                    pool.wait_ge(xn_ready, (nth["ln", st, b] + 1) * NQ)
                    row = ROWS[:, c:c + D].unsqueeze(1).to_broadcast([128, NQ, D])
                    finish(pool.tensor_tensor(X[:, b], X[:, b], row, ALU.add), pre_added)

            pool.wait_ge(preset, 16)
            pool.wait_ge(slot_ready, 1)
            pool.wait_ge(b2_ready, B)
            for i in range(TILES):
                pool.indirect_dma_start(slots, bass.IndirectOffsetOnAxis(ap=slot[:, i:i + 1], axis=0), ROW[:, i], None,
                                        bounds_check=NS * 128 - 1, oob_is_err=False).then_inc(rows_sent, 16)
            for t in range(NS):
                pool.wait_ge(z_ready, t + 1)
                pool.indirect_dma_start(out, bass.IndirectOffsetOnAxis(ap=token[:, t:t + 1], axis=0), XS[:, t, 0:D], None,
                                        bounds_check=B * S - 1, oob_is_err=False).then_inc(stored, 16)
            pool.wait_ge(stored, 16 * NS)

        @block.scalar
        def _(act):
            act.dma_start(CTX[:, :, :], ctx3).then_inc(in_ctx, 16)
            act.dma_start(CON[:, :], consts).then_inc(in_con, 16)
            act.dma_start(ROWS[:, :], rows.partition_broadcast(128)).then_inc(in_small, 16)
            act.dma_start(TAU[:, :], tau.partition_broadcast(128)).then_inc(in_small, 16)
            act.dma_start(DEL[ONES:KR, :], delta.partition_broadcast(KR - ONES)).then_inc(in_small, 16)
            for i in range(3):
                act.dma_start(LB[32 * i:32 * i + 32, :], loraB).then_inc(in_lb, 16)
            act.dma_start(SW[:, :], sw).then_inc(in_moe, 16)
            act.dma_start(B1[:, :], b1).then_inc(in_moe, 16)
            act.dma_start(B2[:, :], b2).then_inc(in_moe, 16)
            act.preload_act_table_set("natural_log_exp_and_others")
            chain = 0
            act.wait_ge(zeroed, 1)
            for s in steps:
                kind = s[0]
                if kind == "ln":
                    _, st, b = s
                    act.wait_ge(stats_ready, (nth[s] + 1) * NQ)
                    act.activation(logvar[:, b], mean_var[:, b, :, 1], ACT.Ln, bias=eps[:, :]).then_inc(act_chain, 1)
                    chain += 1
                    act.wait_ge(act_chain, chain)
                    act.activation(rstd[:, b], logvar[:, b], ACT.Exp, scale=-0.5).then_inc(rstd_ready, 1)
                elif kind == "xt":
                    _, st, b = s
                    read(act, s)
                    act.activation(XNT[:, b], bank(s)[:, :], ACT.Identity).then_inc(xnt_ready, 1)
                elif kind == "kp":
                    l = s[1]
                    act.wait_ge(in_att[l], 16)
                    for g in range(G):
                        key = (*s, g // 2)
                        read(act, key)
                        ps = bank(key)[0:QR, (g % 2) * B * KEYS:(g % 2 + 1) * B * KEYS].rearrange("p (b k) -> p b k", b=B)
                        ins = act.activation(Kf[:, g], ps, ACT.Identity, bias=ATT[l][0:QR, A_BK + g:A_BK + g + 1])
                        ins.then_inc(k_biased, 1)
                elif kind == "q":
                    _, l, b = s
                    for g in range(G):
                        read(act, (*s, g))
                        act.activation(QG[0:QR, b, g], bank((*s, g))[0:QR, :], ACT.Identity,
                                       bias=ATT[l][0:QR, A_BQ + g:A_BQ + g + 1]).then_inc(qh_ready, 1)
                elif kind == "mt":
                    _, l, b = s
                    read(act, s)
                    for g in (0, 1):
                        act.activation(QG[ONES:KR, b, g], bank(s)[32 * g:32 * g + KR - ONES, :], ACT.Identity).then_inc(m_act, 1)
                elif kind == "sc":
                    _, l, b, t = s
                    n = (2 * l + b) * 2 * NT + t
                    w = WIDTHS[t % NT]
                    act.wait_ge(scores_ready, n + 1)
                    if n >= NP:
                        act.wait_ge(probs_used, n - NP + 1)
                    act.activation(P[0:w, n % NP], scores[n % 2][0:w, :], ACT.Exp).then_inc(probs_ready, 1)
                elif kind == "ot":
                    _, l, b = s
                    read(act, s)
                    act.activation(OT[:, b], bank(s)[:, :], ACT.Identity, bias=ATT[l][:, A_BV:A_BV + 1]).then_inc(ot_ready, 1)
                elif kind == "hid":
                    _, b, k = s
                    if k % 2 == 0:
                        read(act, s)
                        act.activation(HT[:, b, k], bank(s)[:, :], ACT.Relu,
                                       bias=W0[:, W_WIB + k:W_WIB + k + 1]).then_inc(hid_act, 1)
                elif kind == "route":
                    b = s[1]
                    act.wait_ge(lg_ready, b + 1)
                    act.activation(ex[:, b], lg[:, b], ACT.Exp).then_inc(ex_ready, 1)
                elif kind == "ct":
                    b = s[1]
                    read(act, s)
                    act.activation(CT[:, b], bank(s)[0:E, :], ACT.Identity).then_inc(ct_ready, 1)

            def transposed(t):
                act.wait_ge(xst_full, t + 1)
                act.activation(XST[:, t % 2], maxps[t % 2][:, 0:128], ACT.Identity).then_inc(xst_ready, 1)

            for t in range(-1, NS):
                if t + 1 < NS:
                    transposed(t + 1)
                if t >= 0:
                    act.wait_ge(biased, t + 1)
                    if t >= NHB:
                        act.wait_ge(y_full, t - NHB + 1)
                    act.activation(HG1[:, t % NHB], HB[:, t % 2], ACT.Gelu_apprx_tanh).then_inc(gelu_ready, 1)

        @block.vector
        def _(dve):
            chain = [0]

            def link(ins):
                chain[0] += 1
                ins.then_inc(dve_chain, 1)
                dve.wait_ge(dve_chain, chain[0])

            for s in steps:
                kind = s[0]
                if kind == "ln":
                    _, st, b = s
                    if st == 0:
                        dve.wait_ge(in_x[b], 16)
                    for t in range(NQ):
                        ins = dve.bn_stats(stats[:, b, t], X[:, b, t])
                    link(ins)
                    for t in range(NQ):
                        dve.bn_aggr(mean_var[:, b, t], stats[:, b, t]).then_inc(stats_ready, 1)
                    dve.wait_ge(stats_ready, (nth[s] + 1) * NQ)
                    dve.wait_ge(rstd_ready, nth[s] + 1)
                    for t in range(NQ):
                        xn = ROW[:, b * NQ + t, D:2 * D] if st == 3 else XN[:, b, t]
                        dve.tensor_scalar(xn, X[:, b, t], mean_var[:, b, t, 0:1], rstd[:, b, t:t + 1],
                                          ALU.subtract, ALU.mult).then_inc(xn_ready, 1)
                elif kind == "kp":
                    l = s[1]
                    dve.wait_ge(tau_ready, 1)
                    dve.wait_ge(k_biased, G * (l + 1))
                    if l == 1:
                        dve.wait_ge(kg_ready, G * B)
                    for b in range(B):
                        ins = dve.tensor_scalar(Kt[:, :, b], Kf[:, :, b], tau8[0:QR, b:b + 1], None, ALU.mult)
                    link(ins)
                    link(dve.tensor_copy(Ks[:, :, :, :], Kt[:, :, :, :]))
                    dve.tensor_tensor(Ks[32:64], Kt[32:64], Ks[32:64].bitcast(F32), ALU.subtract).then_inc(k_split, 1)
                elif kind == "vp":
                    _, l, b, j = s
                    read(dve, s)
                    if (l, b, j) == (0, 0, 0):
                        dve.wait_ge(in_con, 16)
                    w = WIDTHS[j]
                    o = VP[0:w, l, b, j, :, 0:HALF * VC].rearrange("p s (h c) -> p s h c", c=VC)[:, :, :, 0:DK]
                    v = bank(s)[0:w, 0:D].rearrange("p (s h c) -> p s h c", s=2, c=DK)
                    m = CON[0:w, C_VM + HALF * j:C_VM + HALF * (j + 1)].unsqueeze(1).unsqueeze(3).to_broadcast([w, 2, HALF, DK])
                    dve.tensor_tensor(o, v, m, ALU.mult).then_inc(v_ready, 1)
                elif kind == "q":
                    _, l, b = s
                    n = 2 * l + b
                    for g in range(G):
                        dve.wait_ge(qh_ready, G * n + g + 1)
                        dve.scalar_tensor_tensor(QG[64:96, b, g], bank((*s, g))[64:96, :], ATT[l][64:96, A_BQ + g:A_BQ + g + 1],
                                                 QG[64:96, b, g].bitcast(F32), ALU.add, ALU.subtract).then_inc(ql_ready, 1)
                elif kind == "max":
                    _, l, b, i = s
                    n = (2 * l + b) * NQ * G + i
                    qt, g = divmod(i, G)
                    dve.wait_ge(max_full, n + 1)
                    dve.tensor_reduce(MR[:, b, qt, g, 2:2 + HG],
                                      maxps[n % 2][:, 0:GK].rearrange("p (h k) -> p h k", h=HG),
                                      AX.X, ALU.max).then_inc(max_read, 1)
                elif kind == "mt":
                    _, l, b = s
                    read(dve, s)
                    for g in (2, 3):
                        dve.tensor_copy(QG[ONES:KR, b, g], bank(s)[32 * g:32 * g + KR - ONES, :]).then_inc(m_dve, 1)
                elif kind == "on":
                    _, l, b = s
                    n = 2 * l + b
                    dve.wait_ge(probs_used, 2 * NT * (n + 1))
                    for i in range(2):
                        o = acc[i][:, 0:4 * HALF * VC].rearrange("p (t h c) -> p t h c", t=2, c=VC)
                        ins = dve.reciprocal(rden[:, b, 2 * i:2 * i + 2], o[:, :, :, DK])
                    link(ins)
                    for i in range(2):
                        o = acc[i][:, 0:4 * HALF * VC].rearrange("p (t h c) -> p t h c", t=2, c=VC)
                        rd = rden[:, b, 2 * i:2 * i + 2].unsqueeze(3).to_broadcast([128, 2, H, DK])
                        dve.tensor_tensor(ON[:, b, 2 * i:2 * i + 2].rearrange("p t (h c) -> p t h c", c=DK),
                                          o[:, :, :, 0:DK], rd, ALU.mult).then_inc(on_ready, 1)
                elif kind == "b2":
                    b = s[1]
                    read(dve, s)
                    dve.tensor_tensor(ROW[:, b * NQ:(b + 1) * NQ, 0:D], X[:, b], bank(s)[:, :].rearrange("p (t d) -> p t d", t=NQ),
                                      ALU.add).then_inc(b2_ready, 1)
                elif kind in ("wo", "out"):
                    b = s[-1]
                    st = 1 if kind == "out" else 2 * s[1]
                    dve.wait_ge(pre_added, nth["pre", st, b] + 1)
                    read(dve, s)
                    dve.tensor_tensor(X[:, b], X[:, b], bank(s)[:, :].rearrange("p (t d) -> p t d", t=NQ),
                                      ALU.add).then_inc(x_ready, 1)
                    dve.wait_ge(x_ready, nth[s] + 1)
                elif kind in ("gate", "route"):
                    b = s[1]
                    width = E + E * R if kind == "gate" else E
                    c = R_GB if kind == "gate" else R_SB
                    read(dve, s)
                    ps = bank(s)[:, 0:NQ * width].rearrange("p (t e) -> p t e", t=NQ)
                    gb = ROWS[:, c:c + E].unsqueeze(1).to_broadcast([128, NQ, E])
                    link(dve.tensor_tensor(lg[:, b], ps[:, :, 0:E], gb, ALU.add))
                    link(dve.tensor_reduce(lmax[:, b], lg[:, b], AX.X, ALU.max))
                    mb = lmax[:, b].unsqueeze(2).to_broadcast([128, NQ, E])
                    link(dve.tensor_tensor(eq[:, b], lg[:, b], mb, ALU.is_equal))
                    if kind == "route":
                        dve.tensor_tensor(lg[:, b], lg[:, b], mb, ALU.subtract).then_inc(lg_ready, 1)
                    ew = CON[:, C_EW:C_EW + E].unsqueeze(1).to_broadcast([128, NQ, E])
                    link(dve.tensor_tensor(eq[:, b], eq[:, b], ew, ALU.mult))
                    link(dve.tensor_reduce(first[:, b], eq[:, b], AX.X, ALU.max))
                    fb = first[:, b].unsqueeze(2).to_broadcast([128, NQ, E])
                    link(dve.tensor_tensor(hot[:, b], eq[:, b], fb, ALU.is_equal))
                    if kind == "route":
                        dve.tensor_copy(hotb[:, b * NQ:(b + 1) * NQ], hot[:, b]).then_inc(hot_ready, 1)
                    if kind == "gate":
                        for i in range(3):
                            for t in range(NQ):
                                o = U3[:, b, t, 32 * i:32 * i + 32].rearrange("p (e r) -> p e r", r=R)
                                u = ps[:, t, E:].rearrange("p (e r) -> p e r", r=R)
                                hb = hot[:, b, t].unsqueeze(2).to_broadcast([128, E, R])
                                dve.tensor_tensor(o, u, hb, ALU.mult).then_inc(u3_ready, 1)
                    else:
                        dve.wait_ge(ex_ready, b + 1)
                        link(dve.tensor_reduce(esum[:, b], ex[:, b], AX.X, ALU.add))
                        link(dve.reciprocal(esum[:, b], esum[:, b]))
                        pb = esum[:, b].unsqueeze(2).to_broadcast([128, NQ, E])
                        dve.tensor_tensor(coef[:, b], hot[:, b], pb, ALU.mult).then_inc(coef_ready, 1)
                        dve.wait_ge(rows_set, 1)
                        dve.tensor_copy(ROW[:, b * NQ:(b + 1) * NQ, R_P], esum[:, b])
                elif kind == "ut":
                    b = s[1]
                    if b == 0:
                        dve.wait_ge(in_lb, 48)
                        link(dve.tensor_copy(LS[:, :], LB[0:QR, :]))
                        dve.tensor_tensor(LS[32:64], LB[32:64], LS[32:64].bitcast(F32), ALU.subtract).then_inc(lb_ready, 1)
                    read(dve, s)
                    link(dve.tensor_copy(U[:, b], bank(s)[0:QR, :]))
                    dve.tensor_tensor(U[64:96, b], bank(s)[64:96, :], U[64:96, b].bitcast(F32), ALU.subtract).then_inc(u_ready, 1)
                elif kind == "hid":
                    _, b, k = s
                    if k % 2 == 1:
                        read(dve, s)
                        dve.tensor_scalar(HT[:, b, k], bank(s)[:, :], W0[:, W_WIB + k:W_WIB + k + 1], 0.0,
                                          ALU.add, ALU.max).then_inc(hid_dve, 1)
                elif kind == "rank":
                    read(dve, s)
                    before_me = bank(s)[:, 0:TILES * E].rearrange("p (t e) -> p t e", e=E)
                    count = bank(s)[:, TILES * E:TILES * E + E]
                    thr = CON[:, C_THR:C_THR + TILES].unsqueeze(1).to_broadcast([128, E, TILES])
                    link(dve.tensor_tensor(above[:, :, :], count.unsqueeze(2).to_broadcast([128, E, TILES]), thr, ALU.is_gt))
                    link(dve.tensor_reduce(tiles_of[:, :], above[:, :, :], AX.X, ALU.add))
                    low = CON[:, C_LOW:C_LOW + E * E].rearrange("p (e f) -> p e f", f=E)
                    link(dve.tensor_tensor(lower[:, :, :], low, tiles_of[:, :].unsqueeze(1).to_broadcast([128, E, E]), ALU.mult))
                    link(dve.tensor_reduce(first_tile[:, :], lower[:, :, :], AX.X, ALU.add))
                    link(dve.scalar_tensor_tensor(place[:, :, :], first_tile[:, :].unsqueeze(1).to_broadcast([128, TILES, E]), 128.0,
                                                  before_me, ALU.mult, ALU.add))
                    link(dve.tensor_tensor(place[:, :, :], place[:, :, :], hot[:, :, :, :].rearrange("p b t e -> p (b t) e"), ALU.mult))
                    link(dve.tensor_reduce(slot_f[:, :], place[:, :, :], AX.X, ALU.add))
                    dve.tensor_copy(slot[:, :], slot_f[:, :]).then_inc(slot_ready, 1)
                    link(dve.tensor_tensor(end_tile[0:1, :], first_tile[0:1, :], tiles_of[0:1, :], ALU.add))
                    no = CON[0:1, C_T:C_T + NS].unsqueeze(2).to_broadcast([1, NS, E])
                    link(dve.tensor_tensor(past[:, :, :], no, end_tile[0:1, :].unsqueeze(1).to_broadcast([1, NS, E]), ALU.is_ge))
                    link(dve.tensor_reduce(tile_f[:, 0:NS], past[:, :, :], AX.X, ALU.add))
                    dve.tensor_scalar(tile_e[:, 0:NS], tile_f[:, 0:NS], float(E - 1), None, ALU.min).then_inc(tile_ready, 1)

            dve.wait_ge(tile_ready, 1)
            for e in range(E):
                dve.wait_ge(in_w1[e], 16)
            expert = {}
            for t in range(-1, NS + 2):
                if t + 1 < NS:
                    n = t + 1
                    expert[n] = dve.value_load(tile_e[0:1, n:n + 1], min_val=0, max_val=E - 1)
                    if n >= 2:
                        dve.wait_ge(hidden_full, n - 1)
                    dve.tensor_copy(W1C[:, n % 2], W1[:, bass.ds(expert[n] * F, F)]).then_inc(w1_ready, 1)
                if 0 <= t < NS:
                    dve.wait_ge(hidden_full, t + 1)
                    if t >= 2:
                        dve.wait_ge(gelu_ready, t - 1)
                    bias = B1[:, bass.ds(expert[t] * NF, NF)].unsqueeze(2).to_broadcast([128, NF, 128])
                    dve.tensor_tensor(HB[:, t % 2].rearrange("p (k n) -> p k n", k=NF),
                                      hidden[t % NHB][:, :].rearrange("p (k n) -> p k n", k=NF), bias, ALU.add).then_inc(biased, 1)
                if t - 2 >= 0:
                    n = t - 2
                    for i, (t0, t1) in enumerate(LOADS):
                        if n == t0:
                            dve.wait_ge(slots_in[i], 16)
                            dve.tensor_copy(token[:, t0:t1], XS[:, t0:t1, R_ID])
                    dve.wait_ge(y_full, n + 1)
                    dve.scalar_tensor_tensor(XS[:, n, 0:D], acc[n % 2][:, 0:D], XS[:, n, R_P:R_P + 1], XS[:, n, 0:D],
                                             ALU.mult, ALU.add).then_inc(z_ready, 1)

        @block.tensor
        def _(pe):
            def hold(key):
                if key in before:
                    by = reader(before[key])
                    for signal, value in by if isinstance(by, list) else [by]:
                        pe.wait_ge(signal, value)

            done = full
            for s in steps:
                kind = s[0]
                if kind == "xt":
                    _, st, b = s
                    if nth[s] == 0:
                        pe.wait_ge(in_con, 16)
                    hold(s)
                    pe.wait_ge(xn_ready, NQ * (nth["ln", st, b] + 1))
                    for t in range(NQ):
                        xn = ROW[:, b * NQ + t, D:2 * D] if st == 3 else XN[:, b, t]
                        ins = pe.transpose(bank(s)[:, 128 * t:128 * t + 128], xn, ident)
                    ins.then_inc(done[use[s][0]], 1)
                elif kind == "kp":
                    l = s[1]
                    pe.wait_ge(in_att[l], 16)
                    pe.wait_ge(in_ctx, 16)
                    for g in range(G):
                        key = (*s, g // 2)
                        if g % 2 == 0:
                            hold(key)
                        ins = pe.matmul(bank(key)[0:QR, (g % 2) * B * KEYS:(g % 2 + 1) * B * KEYS].rearrange("p (b k) -> p b k", b=B),
                                        ATT[l][:, A_K + QR * g:A_K + QR * (g + 1)], CTX[:, :, 0:KEYS], start=True, stop=True)
                        if g % 2 == 1:
                            ins.then_inc(done[use[key][0]], 1)
                elif kind == "vp":
                    _, l, b, j = s
                    hold(s)
                    w, k0 = WIDTHS[j], STARTS[j] % KEYS
                    pe.matmul(bank(s)[0:w, 0:D], CTX[:, b, k0:k0 + w], ATT[l][:, A_V:A_V + D],
                              start=True, stop=True).then_inc(done[use[s][0]], 1)
                elif kind == "q":
                    _, l, b = s
                    pe.wait_ge(xnt_ready, nth["xt", 2 * l, b] + 1)
                    for g in range(G):
                        key = (*s, g)
                        hold(key)
                        pe.matmul(bank(key)[0:QR, :], ATT[l][:, A_Q + QR * g:A_Q + QR * (g + 1)], XNT[:, b], start=True,
                                  stop=True).then_inc(done[use[key][0]], 1)
                elif kind == "max":
                    _, l, b, i = s
                    n = nth[s]
                    qt, g = divmod(i, G)
                    if i == 0:
                        pe.wait_ge(ql_ready, G * (nth["q", l, b] + 1))
                        pe.wait_ge(kg_ready, G * (nth["km", l, b] + 1))
                        pe.wait_ge(erows, 6 + G * B)
                    if n >= 2:
                        pe.wait_ge(max_read, n - 1)
                    off = PAD * (g % 2)
                    pe.matmul(maxps[n % 2][:, 0:GK], QG[0:ONES + 2, b, g, 128 * qt:128 * qt + 128],
                              KG[0:ONES + 2, b, g, off:off + GK], start=True, stop=True).then_inc(max_full, 1)
                elif kind == "mt":
                    _, l, b = s
                    hold(s)
                    pe.wait_ge(max_read, NQ * G * (nth[s] + 1))
                    pe.wait_ge(zeroed, 6)
                    for t in range(NQ):
                        ins = pe.transpose(bank(s)[:, 128 * t:128 * t + 128], MR[:, b, t], ident)
                    ins.then_inc(done[use[s][0]], 1)
                elif kind == "sc":
                    _, l, b, t = s
                    n = nth[s]
                    half, j = divmod(t, NT)
                    w = WIDTHS[j]
                    if t == 0:
                        pe.wait_ge(m_act, 2 * (nth["mt", l, b] + 1))
                        pe.wait_ge(m_dve, 2 * (nth["mt", l, b] + 1))
                    if n >= 2:
                        pe.wait_ge(probs_ready, n - 1)
                    parts = {0: [(0, 0)], 1: [(0, 123)], 2: [(0, 246), (1, 0)], 3: [(1, 124)], 4: [(1, 247)]}[j]
                    for i, (odd, c) in enumerate(parts):
                        g = 2 * half + odd
                        ins = pe.matmul(scores[n % 2][0:w, :], KG[:, b, g, c:c + w], QG[:, b, g],
                                        start=(i == 0), stop=(i == len(parts) - 1))
                    ins.then_inc(scores_ready, 1)
                elif kind == "pv":
                    _, l, b, t = s
                    n = nth[s]
                    half, j = divmod(t, NT)
                    w = WIDTHS[j]
                    if t == 0:
                        pe.wait_ge(v_ready, B * NT * (l + 1))
                        pe.wait_ge(ones_col, 8)
                        if n > 0:
                            pe.wait_ge(on_ready, 2 * nth["on", l, b])
                    pe.wait_ge(probs_ready, n + 1)
                    cols = HALF * VC
                    for qt in range(NQ):
                        c = (qt % 2) * 2 * cols + half * cols
                        ins = pe.matmul(acc[qt // 2][:, c:c + VW], P[0:w, n % NP, 128 * qt:128 * qt + 128],
                                        VP[0:w, l, b, j, half],
                                        start=(t == 0 and qt % 2 == 0), stop=(t == 2 * NT - 1 and qt % 2 == 1),
                                        skip_group_check=True)
                    ins.then_inc(probs_used, 1)
                elif kind == "ot":
                    _, l, b = s
                    hold(s)
                    pe.wait_ge(on_ready, 2 * (nth["on", l, b] + 1))
                    for t in range(NQ):
                        ins = pe.transpose(bank(s)[:, 128 * t:128 * t + 128], ON[:, b, t], ident)
                    ins.then_inc(done[use[s][0]], 1)
                elif kind == "wo":
                    _, l, b = s
                    hold(s)
                    pe.wait_ge(ot_ready, nth["ot", l, b] + 1)
                    for t in range(NQ):
                        ins = pe.matmul(bank(s)[:, D * t:D * (t + 1)], OT[:, b, 128 * t:128 * t + 128],
                                        ATT[l][:, A_O:A_O + D], start=True, stop=True)
                    ins.then_inc(done[use[s][0]], 1)
                elif kind in ("gate", "route"):
                    b = s[1]
                    st = 1 if kind == "gate" else 3
                    width = E + E * R if kind == "gate" else E
                    w = W0[:, W_GA:W_GA + width] if kind == "gate" else SW[:, :]
                    if b == 0:
                        pe.wait_ge(*((in_w0, 16) if kind == "gate" else (in_moe, 48)))
                    hold(s)
                    pe.wait_ge(xnt_ready, nth["xt", st, b] + 1)
                    for t in range(NQ):
                        ins = pe.matmul(bank(s)[:, width * t:width * (t + 1)], XNT[:, b, 128 * t:128 * t + 128], w,
                                        start=True, stop=True)
                    ins.then_inc(done[use[s][0]], 1)
                elif kind == "ut":
                    b = s[1]
                    hold(s)
                    pe.wait_ge(u3_ready, 3 * NQ * (nth[s] + 1))
                    for t in range(NQ):
                        ins = pe.transpose(bank(s)[0:QR, 128 * t:128 * t + 128], U3[:, b, t], ident)
                    ins.then_inc(done[use[s][0]], 1)
                elif kind == "hid":
                    _, b, k = s
                    hold(s)
                    pe.matmul(bank(s)[:, :], W0[:, W_WI + 128 * k:W_WI + 128 * (k + 1)], XNT[:, b], start=True, stop=False)
                    if k == 0:
                        pe.wait_ge(u_ready, nth["ut", b] + 1)
                        pe.wait_ge(lb_ready, 1)
                    pe.matmul(bank(s)[:, :], LS[:, 128 * k:128 * (k + 1)], U[:, b], start=False,
                              stop=True).then_inc(done[use[s][0]], 1)
                elif kind == "out":
                    b = s[-1]
                    hold(s)
                    pe.wait_ge(hid_act, 2 * (b + 1))
                    pe.wait_ge(hid_dve, 2 * (b + 1))
                    for t in range(NQ):
                        for k in range(NF):
                            w = W0[:, W_WO + D * k:W_WO + D * (k + 1)]
                            ins = pe.matmul(bank(s)[:, D * t:D * (t + 1)], HT[:, b, k, 128 * t:128 * t + 128], w,
                                            start=(k == 0), stop=(k == NF - 1))
                    ins.then_inc(done[use[s][0]], 1)
                elif kind == "ct":
                    b = s[1]
                    hold(s)
                    pe.wait_ge(coef_ready, b + 1)
                    for t in range(NQ):
                        ins = pe.transpose(bank(s)[0:E, 128 * t:128 * t + 128], coef[:, b, t], ident)
                    ins.then_inc(done[use[s][0]], 1)
                elif kind == "b2":
                    b = s[1]
                    hold(s)
                    pe.wait_ge(ct_ready, b + 1)
                    for t in range(NQ):
                        ins = pe.matmul(bank(s)[:, D * t:D * (t + 1)], CT[:, b, 128 * t:128 * t + 128], B2[:, :],
                                        start=True, stop=True)
                    ins.then_inc(done[use[s][0]], 1)
                elif kind == "rank":
                    hold(s)
                    pe.wait_ge(hot_ready, B)
                    pe.wait_ge(binary, 2)
                    ps = bank(s)
                    pe.matmul(ps[:, 0:TILES * E], trib[:, :], hotb[:, :, :].rearrange("p t e -> p (t e)"), start=True, stop=False,
                              skip_group_check=True)
                    for i in range(TILES):
                        n = TILES - i
                        ins = pe.matmul(ps[:, E * (i + 1):E * (TILES + 1)].rearrange("p (t e) -> p t e", e=E), onesb[:, :],
                                        hotb[:, i].unsqueeze(1).to_broadcast([128, n, E]), start=False, stop=(i == TILES - 1),
                                        skip_group_check=True)
                    ins.then_inc(done[use[s][0]], 1)

            def expert_out(t):
                pe.wait_ge(gelu_ready, t + 1)
                if t >= 2:
                    pe.wait_ge(z_ready, t - 1)
                for k in range(NF):
                    ins = pe.matmul(acc[t % 2][:, 0:D], HG1[:, t % NHB, 128 * k:128 * (k + 1)],
                                    W2[:, bass.ds(expert[t] * (NF * D) + D * k, D)], start=(k == 0), stop=(k == NF - 1))
                ins.then_inc(y_full, 1)

            for e in range(E):
                pe.wait_ge(in_w2[e], 16)
            pe.wait_ge(tile_ready, 1)
            expert = {}
            for t in range(-1, NS + 2):
                if t + 1 < NS:
                    n = t + 1
                    expert[n] = pe.value_load(tile_e[0:1, n:n + 1], min_val=0, max_val=E - 1)
                    for i, (t0, t1) in enumerate(LOADS):
                        if n == t0:
                            pe.wait_ge(slots_in[i], 16)
                    if n >= 2:
                        pe.wait_ge(xst_ready, n - 1)
                    pe.transpose(maxps[n % 2][:, 0:128], XS[:, n, D:2 * D], ident).then_inc(xst_full, 1)
                if 0 <= t < NS:
                    pe.wait_ge(xst_ready, t + 1)
                    pe.wait_ge(w1_ready, t + 1)
                    if t >= NHB:
                        pe.wait_ge(biased, t - NHB + 1)
                    for k in range(NF):
                        ins = pe.matmul(hidden[t % NHB][:, 128 * k:128 * (k + 1)], W1C[:, t % 2, 128 * k:128 * (k + 1)],
                                        XST[:, t % 2], start=True, stop=True)
                    ins.then_inc(hidden_full, 1)
                if t >= 2:
                    expert_out(t - 2)


_INS = ["x", "ctx3", "att0", "att1", "consts", "rows", "delta", "tau", "ffn0w", "loraB", "sw", "w1", "b1", "w2", "b2"]


def constants():
    c = np.zeros((128, C_N), np.float32)
    c[:, C_ID:C_ID + 128] = np.eye(128)
    for j in range(NT):
        for r in range(WIDTHS[j]):
            c[r, C_VM + HALF * j + (STARTS[j] + r) // KEYS] = 1
    for r in range(QR):
        c[r, C_KM + (r % 32) // DK] = 1
    c[:, C_EW:C_EW + E] = np.arange(E, 0, -1)
    c[ONES, C_SEL] = 1
    c[ONES + 1, C_SEL + 1] = 1
    for h in range(HG):
        c[ONES + 2 + h, C_NEG + h] = -1
    p = np.arange(128)
    for t in range(TILES):
        c[:, C_TAIL + 4 * t + 1] = 128 * t + p
    for t in range(NS):
        c[:, C_SID + t] = B * S + 128 * t + p
        c[:, C_T + t] = t
    c[:, C_THR:C_THR + TILES] = 128 * np.arange(TILES)
    c[:, C_LOW:C_LOW + E * E] = np.tri(E, E, -1).reshape(-1)
    c[:, C_TRI:C_TRI + 128] = np.tri(128, 128, -1).T
    return c


def kernel(**inputs):
    import concourse.bacc as _bacc
    from concourse.bass_utils import run_bass_kernel_spmd as _run

    a = {k: np.asarray(v) for k, v in inputs.items()}

    def attention_weights(l):
        p = f"L{l}_xcond_"
        out = np.zeros((128, A_N), np.float32)
        for g in range(G):
            for i in range(3):
                rows_ = slice(32 * g, 32 * g + 32)
                for c, cb, n in ((A_K, A_BK, "k"), (A_Q, A_BQ, "q")):
                    out[:, c + QR * g + 32 * i:c + QR * g + 32 * (i + 1)] = a[p + "W" + n][rows_].T
                    out[32 * i:32 * (i + 1), cb + g] = a[p + "b" + n][rows_]
        out[:, A_V:A_V + D] = a[p + "Wv"].T
        out[:, A_O:A_O + D] = a[p + "Wo"].T
        out[:, A_BV] = a[p + "bv"]
        return out

    ctx_t = a["ctx_1024"].transpose(2, 0, 1)
    f0 = "L0_ffn_"
    by_tile = lambda w: w.reshape(NF, 128, -1).transpose(1, 0, 2).reshape(128, -1)
    arrays = {
        "x": a["x"].reshape(B * S, D),
        "ctx3": np.concatenate([ctx_t] * 3, axis=2),
        "att0": attention_weights(0),
        "att1": attention_weights(1),
        "consts": constants(),
        "rows": np.concatenate([a["L0_xcond_bo"], a[f0 + "wo_b"], a["L1_xcond_bo"], a[f0 + "gate_b"], a["L1_ffn_switch_b"]]),
        "delta": a["fside_BxS2_0"].reshape(-1),
        "tau": a["condB_tau"],
        "ffn0w": np.concatenate([a[f0 + "gate_W"].T, a[f0 + "lora_A"].reshape(E * R, D).T, a[f0 + "wi_W"].T,
                                 by_tile(a[f0 + "wo_W"].T), a[f0 + "wi_b"].reshape(NF, 128).T], axis=1),
        "loraB": a[f0 + "lora_B"].transpose(0, 2, 1).reshape(E * R, F),
        "sw": a["L1_ffn_switch_w"],
        "w1": a["L1_ffn_w1"].transpose(1, 0, 2),
        "b1": a["L1_ffn_b1"].reshape(E, NF, 128).transpose(2, 0, 1).reshape(128, E * NF),
        "w2": a["L1_ffn_w2"].reshape(E, NF, 128, D).transpose(2, 0, 1, 3).reshape(128, E, NF * D),
        "b2": a["L1_ffn_b2"],
    }
    nc = _bacc.Bacc("TRN2", target_bir_lowering=False, num_devices=1)
    feeds, args = {}, []
    for name in _INS:
        v = np.ascontiguousarray(arrays[name])
        feeds[f"in_{name}"] = v
        args.append(nc.dram_tensor(f"in_{name}", v.shape, mybir.dt.from_np(v.dtype), kind="ExternalInput").ap())
    out = nc.dram_tensor("out", (B * S, D), F32, kind="ExternalOutput").ap()
    build(nc, *args, out)
    r = _run(nc, [feeds], core_ids=[0])
    return r.results[0]["out"].reshape(B, S, D)
```

```python
from contextlib import ExitStack

import numpy as np
import concourse.bass as bass
from concourse import mybir

F32 = mybir.dt.float32
F32R = mybir.dt.float32r
BF16 = mybir.dt.bfloat16
I32 = mybir.dt.int32
ALU = mybir.AluOpType
ACT = mybir.ActivationFunctionType
AX = mybir.AxisListType

B = 2
S = 512
D = 128
NQ = S // 128
KEYS = 77
H = 16
DK = D // H
G = 4
HG = H // G
GK = HG * KEYS
HALF = 8
NT = 5
STARTS = [0, 123, 246, 370, 493]
WIDTHS = [123, 123, 124, 123, 123]
TW = 124
GP = 370
PAD = GP - GK
QR = 3 * 32
ONES = QR
KR = QR + 2 + HG
VC = DK + 1
VW = 128
E = 8
R = 4
F = 512
NF = F // 128
EPS = 1e-5
TILES = B * NQ
NSB = NQ + E - 1
NS = B * NSB
RW = 2 * D + 4
R_P, R_ID = 2 * D, 2 * D + 1
LOADS = [(0, 1), (1, 3), (3, 6), (6, NSB)]
NHB = 3
RS8 = 1.0 / float(np.sqrt(np.float32(DK)))

A_K, A_Q, A_V, A_O = 0, G * QR, 2 * G * QR, 2 * G * QR + D
A_BK = A_O + D
A_BQ = A_BK + G
A_BV = A_BQ + G
A_N = A_BV + 1
C_ID = 0
C_VM = C_ID + 128
C_KM = C_VM + NT * HALF
C_EW = C_KM + HG
C_SEL = C_EW + E
C_TAIL = C_SEL + 3
C_SID = C_TAIL + 4 * TILES
C_THR = C_SID + NS
C_LOW = C_THR + NQ
C_T = C_LOW + E * E
C_TRI = C_T + NSB
C_N = C_TRI + 128
R_BO0, R_WOB, R_BO1, R_GB, R_SB = 0, D, 2 * D, 3 * D, 3 * D + E
R_N = R_SB + E
W_GA, W_WI, W_WO = 0, E + E * R, E + E * R + F
W_WIB = W_WO + NF * D
W_N = W_WIB + NF


def schedule():
    table = """
        ln/0/0 vp/0/0/0 xt/0/0 ln/0/1 kp/0 xt/0/1 q/0/0/0:4 km/0/0 max/0/0/0:5 vp/0/0/1 max/0/0/5 vp/0/0/2:5 vp/0/1/0
        max/0/0/6 q/0/1/0:2 vp/0/1/1 max/0/0/7:9 q/0/1/2 mt/0/0/0 vp/0/1/2 sc/0/0/0 max/0/0/9:11 pv/0/0/0 km/0/1
        max/0/0/11 vp/0/1/3 sc/0/0/1 max/0/0/12 sc/0/0/2 pv/0/0/1 max/0/0/13 vp/0/1/4 max/0/0/14 pv/0/0/2 max/0/0/15
        sc/0/0/3 q/0/1/3 sc/0/0/4 mt/0/0/1 max/0/1/0:2 pv/0/0/3:5 sc/0/0/5 max/0/1/2 sc/0/0/6 pv/0/0/5:7 sc/0/0/7
        max/0/1/3 sc/0/0/8 max/0/1/4 pv/0/0/7 sc/0/0/9 pv/0/0/8 max/0/1/5 vp/1/0/0 pv/0/0/9 max/0/1/6:8 on/0/0
        mt/0/1/0 max/0/1/8 ot/0/0 max/0/1/9 sc/0/1/0:2 kp/1 pv/0/1/0 sc/0/1/2 pv/0/1/1 max/0/1/10 wo/0/0 max/0/1/11:15
        vp/1/0/1 max/0/1/15 ln/1/0 sc/0/1/3 pv/0/1/2 mt/0/1/1 pv/0/1/3 vp/1/0/2 sc/0/1/4:6 xt/1/0 pv/0/1/4 gate/0
        vp/1/0/3 sc/0/1/6 ut/0 pv/0/1/5 sc/0/1/7 hid/0/0 vp/1/0/4 pv/0/1/6 vp/1/1/0 pv/0/1/7 vp/1/1/1 hid/0/1 km/1/0
        hid/0/2:4 sc/0/1/8 out/0 ln/2/0 vp/1/1/2 pv/0/1/8 sc/0/1/9 pv/0/1/9 xt/2/0 vp/1/1/3 on/0/1 q/1/0/0:2 max/1/0/0
        ot/0/1 max/1/0/1:3 q/1/0/2:4 wo/0/1 max/1/0/3:5 ln/1/1 max/1/0/5:8 vp/1/1/4 max/1/0/8 mt/1/0/0 max/1/0/9
        xt/1/1 sc/1/0/0 max/1/0/10:12 gate/1 max/1/0/12 sc/1/0/1 pv/1/0/0:2 sc/1/0/2 ut/1 km/1/1 hid/1/0 sc/1/0/3
        max/1/0/13 hid/1/1 max/1/0/14 hid/1/2 max/1/0/15 pv/1/0/2 mt/1/0/1 hid/1/3 sc/1/0/4 pv/1/0/3 out/1 sc/1/0/5
        pv/1/0/4 sc/1/0/6 pv/1/0/5 ln/2/1 pv/1/0/6 sc/1/0/7 xt/2/1 q/1/1/0:2 sc/1/0/8 max/1/1/0:2 q/1/1/2 max/1/1/2
        pv/1/0/7 sc/1/0/9 max/1/1/3 q/1/1/3 pv/1/0/8 max/1/1/4:9 mt/1/1/0 pv/1/0/9 max/1/1/9 on/1/0 sc/1/1/0
        max/1/1/10:12 ot/1/0 sc/1/1/1 max/1/1/12 pv/1/1/0 max/1/1/13:15 pv/1/1/1 sc/1/1/2 max/1/1/15 pv/1/1/2 sc/1/1/3
        mt/1/1/1 wo/1/0 pv/1/1/3 sc/1/1/4:6 ln/3/0 pv/1/1/4:6 sc/1/1/6 xt/3/0 sc/1/1/7 route/0 pv/1/1/6 sc/1/1/8
        pv/1/1/7 sc/1/1/9 pv/1/1/8 ct/0 pv/1/1/9 on/1/1 b2/0 rank/0 ot/1/1 wo/1/1 ln/3/1 moe/-1 xt/3/1 moe/0:2 route/1
        moe/2 ct/1 moe/3 rank/1 moe/4 b2/1
    """
    steps = []
    for entry in table.split():
        kind, *index = entry.split("/")
        *outer, last = index
        if ":" in last:
            first, end = last.split(":")
            steps += [(kind, *(int(i) for i in outer), i) for i in range(int(first), int(end))]
        else:
            steps.append((kind, *(int(i) for i in index)))
    return steps + [("moe", t) for t in range(5, NS + 2)]


def order(steps):
    counts, nth = {}, {}
    for s in steps:
        kind = "x" if s[0] in ("wo", "out") else s[0]
        nth[s] = counts[kind] = counts.get(kind, -1) + 1
        if s[0] == "xt" and s[1] < 3:
            nth["pre", s[1], s[2]] = counts["pre"] = counts.get("pre", -1) + 1
    return nth


def banks(steps):
    uses = {}
    for s in steps:
        kind = s[0]
        keys = []
        if kind == "kp":
            keys = [(*s, 0), (*s, 1)]
        elif kind in ("q", "xt", "vp", "mt", "ot", "wo", "gate", "ut", "hid", "out", "route", "ct", "b2", "rank"):
            keys = [s]
        for k in keys:
            n = len(uses)
            uses[k] = (n % 2, n // 2)
    return uses


def build(nc, x, ctx3, att0, att1, consts, rows, delta, tau, ffn0w, loraB, sw, w1, b1, w2, b2, out):
    steps = schedule()
    use = banks(steps)
    nth = order(steps)
    before = {}
    for i in range(2):
        mine = [k for k in use if use[k][0] == i]
        before.update(zip(mine[1:], mine))
    stages = ExitStack()
    with stages:
        def sb(name, shape, dt=F32):
            return stages.enter_context(nc.sbuf_tensor(name, shape, dt))

        def sem(name):
            return stages.enter_context(nc.semaphore(name))

        X = sb("X", [128, B, NQ, D])
        CTX = sb("CTX", [128, B, 3 * KEYS])
        ATT = [sb(f"ATT{l}", [128, A_N]) for l in range(2)]
        CON = sb("CON", [128, C_N])
        ROWS = sb("ROWS", [128, R_N])
        DEL = sb("DEL", [128, B * KEYS])
        TAU = sb("TAU", [128, B])
        W0 = sb("W0", [128, W_N])
        LB = sb("LB", [128, F])
        SW = sb("SW", [128, E])
        W1 = sb("W1", [128, E * F])
        B1 = sb("B1", [128, E * NF])
        W2 = sb("W2", [128, E * NF * D])
        B2 = sb("B2", [E, D])

        stats = sb("stats", [128, B, NQ, 6])
        mean_var = sb("mean_var", [128, B, NQ, 2])
        logvar = sb("logvar", [128, B, NQ])
        rstd = sb("rstd", [128, B, NQ])
        eps = sb("eps", [128, 1])
        XN = sb("XN", [128, B, NQ, D])
        XNT = sb("XNT", [128, B, S])
        tau8 = sb("tau8", [128, B])
        dscaled = sb("dscaled", [128, B * KEYS])
        dhigh = sb("dhigh", [128, B * KEYS], F32R)
        dlow = sb("dlow", [128, B * KEYS])
        Kf = sb("Kf", [QR, G, B, KEYS])
        Kt = sb("Kt", [QR, G, B, KEYS])
        Ks = sb("Ks", [KR, G, B, KEYS], F32R)
        KG = sb("KG", [KR, B, G, GP], F32R)
        VP = sb("VP", [TW, 2, B, NT, 2, VW])
        QG = sb("QG", [KR, B, G, S], F32R)
        MR = sb("MR", [128, B, NQ, G, 32])
        NP = 3
        P = sb("P", [TW, NP, S])
        rden = sb("rden", [128, B, NQ, H])
        ON = sb("ON", [128, B, NQ, D])
        OT = sb("OT", [128, B, S])
        lg = sb("lg", [128, B, NQ, E])
        lmax = sb("lmax", [128, B, NQ])
        eq = sb("eq", [128, B, NQ, E])
        first = sb("first", [128, B, NQ])
        hot = sb("hot", [128, B, NQ, E])
        U3 = sb("U3", [128, B, NQ, QR])
        U = sb("U", [QR, B, S], F32R)
        LS = sb("LS", [QR, F], F32R)
        HT = sb("HT", [128, B, NF, S])
        ROW = sb("ROW", [128, TILES, RW])
        hotb = sb("hotb", [128, TILES, E], BF16)
        trib = sb("trib", [128, 128], BF16)
        onesb = sb("onesb", [128, 128], BF16)
        above = sb("above", [128, E, NQ])
        tiles_of = sb("tiles_of", [128, E])
        lower = sb("lower", [128, E, E])
        first_tile = sb("first_tile", [128, E])
        end_tile = sb("end_tile", [128, E])
        place = sb("place", [128, NQ, E])
        slot_f = sb("slot_f", [128, NQ])
        slot = sb("slot", [128, TILES], I32)
        past = sb("past", [1, NSB, E])
        tile_f = sb("tile_f", [1, NSB])
        tile_e = sb("tile_e", [1, NS], I32)
        XS = sb("XS", [128, NS, RW])
        XST = sb("XST", [128, 2, 128])
        spare = HT[:, :, :, :].rearrange("p b k n -> p (b k) n")
        W1C, HB, HG1 = spare[:, 0:2], spare[:, 2:4], spare[:, 4:4 + NHB]
        token = sb("token", [128, NS], I32)
        slots = nc.dram_tensor("slots", (NS * 128, RW), F32).ap()
        ex = sb("ex", [128, B, NQ, E])
        esum = sb("esum", [128, B, NQ])
        coef = sb("coef", [128, B, NQ, E])
        CT = OT[0:E]

        scores = [stages.enter_context(nc.psum_tensor(f"scores{i}", [128, 512], F32)) for i in range(2)]
        maxps = [stages.enter_context(nc.psum_tensor(f"maxps{i}", [128, 512], F32)) for i in range(2)]
        acc = [stages.enter_context(nc.psum_tensor(f"acc{i}", [128, 512], F32)) for i in range(2)]
        shared = [stages.enter_context(nc.psum_tensor(f"shared{i}", [128, 512], F32)) for i in range(2)]

        in_x = [sem(f"in_x{b}") for b in range(B)]
        in_ctx, in_con, in_small, in_w0, in_lb = sem("in_ctx"), sem("in_con"), sem("in_small"), sem("in_w0"), sem("in_lb")
        in_att = [sem(f"in_att{l}") for l in range(2)]
        in_moe, in_rows = sem("in_moe"), sem("in_rows")
        in_w1 = [sem(f"in_w1_{e}") for e in range(E)]
        in_w2 = [sem(f"in_w2_{e}") for e in range(E)]
        zeroed = sem("zeroed")
        erows = sem("erows")
        ones_col = sem("ones_col")
        pre_added = sem("pre_added")
        k_scaled = sem("k_scaled")
        kg_dve = sem("kg_dve")
        kg_pool = sem("kg_pool")
        full = [sem(f"full{i}") for i in range(2)]
        stats_ready = sem("stats_ready")
        rstd_ready = sem("rstd_ready")
        act_chain = sem("act_chain")
        dve_chain = sem("dve_chain")
        xn_ready = sem("xn_ready")
        xnt_ready = sem("xnt_ready")
        k_biased = sem("k_biased")
        k_split = sem("k_split")
        tau_ready = sem("tau_ready")
        v_ready = sem("v_ready")
        qh_ready = sem("qh_ready")
        ql_ready = sem("ql_ready")
        m_act = sem("m_act")
        m_dve = sem("m_dve")
        max_full = sem("max_full")
        max_read = sem("max_read")
        scores_ready = sem("scores_ready")
        probs_ready = sem("probs_ready")
        probs_used = sem("probs_used")
        on_ready = sem("on_ready")
        ot_ready = sem("ot_ready")
        x_ready = sem("x_ready")
        u3_ready = sem("u3_ready")
        u_ready = sem("u_ready")
        lb_ready = sem("lb_ready")
        hid_act = sem("hid_act")
        hid_dve = sem("hid_dve")
        lg_ready = sem("lg_ready")
        ex_ready = sem("ex_ready")
        coef_ready = sem("coef_ready")
        ct_ready = sem("ct_ready")
        b2_ready = sem("b2_ready")
        preset = sem("preset")
        rows_set = sem("rows_set")
        blank = sem("blank")
        hot_ready = sem("hot_ready")
        binary = sem("binary")
        rank_read = sem("rank_read")
        slot_ready = sem("slot_ready")
        tile_ready = sem("tile_ready")
        rows_sent = [sem(f"rows_sent{b}") for b in range(B)]
        slots_in = [[sem(f"slots_in{b}_{i}") for i in range(len(LOADS))] for b in range(B)]
        xst_full = sem("xst_full")
        xst_ready = sem("xst_ready")
        w1_ready = sem("w1_ready")
        hidden_full = sem("hidden_full")
        biased = sem("biased")
        gelu_ready = sem("gelu_ready")
        y_full = sem("y_full")
        z_ready = sem("z_ready")
        token_ready = sem("token_ready")
        stored = sem("stored")

        ident = CON[:, C_ID:C_ID + 128]
        hidden = scores

        def bank(key):
            return shared[use[key][0]]

        def xst_ps(t):
            return maxps[t % 2][:, 0:128]

        def masked_k(b, odd):
            off = PAD * odd
            o = KG[:, b, odd::2, off:off + GK].rearrange("p g (h k) -> p g h k", h=HG)
            k4 = Ks[:, odd::2, b].bitcast(F32).unsqueeze(2).to_broadcast([KR, G // 2, HG, KEYS])
            m4 = CON[0:KR, C_KM:C_KM + HG].unsqueeze(1).unsqueeze(3).to_broadcast([KR, G // 2, HG, KEYS])
            return o, k4, m4

        def reader(key):
            kind = key[0]
            if kind == "kp":
                return k_biased, G * key[1] + 2 * (key[2] + 1)
            if kind == "q":
                return ql_ready, nth[key] + 1
            if kind == "mt":
                return [(m_act, nth[key] + 1), (m_dve, nth[key] + 1)]
            if kind == "gate":
                return u3_ready, 3 * (nth[key] + 1)
            if kind == "hid":
                return (hid_dve if key[2] % 2 else hid_act), 2 * key[1] + key[2] // 2 + 1
            by = {"xt": xnt_ready, "vp": v_ready, "ot": ot_ready, "route": lg_ready, "rank": tile_ready,
                  "ut": u_ready, "ct": ct_ready, "wo": x_ready, "out": x_ready, "b2": b2_ready}
            return by[kind], nth[key] + 1

        def read(eng, key):
            i, n = use[key]
            eng.wait_ge(full[i], n + 1)

        block = stages.enter_context(nc.Block())

        @block.sync
        def _(sp):
            xv = x.rearrange("(b t p) d -> b p t d", b=B, p=128)
            sp.dma_start(X[:, 0], xv[0]).then_inc(in_x[0], 16)
            sp.dma_start(ATT[0][:, 0:A_Q], att0[:, 0:A_Q]).then_inc(in_att[0], 16)
            sp.dma_start(ATT[0][:, A_Q:], att0[:, A_Q:]).then_inc(in_att[0], 16)
            sp.dma_start(DEL[ONES:KR, :], delta.partition_broadcast(KR - ONES)).then_inc(in_small, 16)
            sp.dma_start(X[:, 1], xv[1]).then_inc(in_x[1], 16)
            sp.dma_start(ROWS[:, :], rows.partition_broadcast(128)).then_inc(in_rows, 16)
            sp.dma_start(W0[:, :], ffn0w).then_inc(in_w0, 16)
            for i in range(3):
                sp.dma_start(LB[32 * i:32 * i + 32, :], loraB).then_inc(in_lb, 16)
            sp.dma_start(ATT[1][:, :], att1).then_inc(in_att[1], 16)
            sp.dma_start(SW[:, :], sw).then_inc(in_moe, 16)
            sp.dma_start(B1[:, :], b1).then_inc(in_moe, 16)
            sp.dma_start(B2[:, :], b2).then_inc(in_moe, 16)
            for e in range(E):
                sp.dma_start(W1[:, e * F:(e + 1) * F], w1[:, e]).then_inc(in_w1[e], 16)
                sp.dma_start(W2[:, e * NF * D:(e + 1) * NF * D], w2[:, e]).then_inc(in_w2[e], 16)
            sv = slots.rearrange("(t p) w -> p t w", p=128)
            sp.wait_ge(blank, 2)
            sp.dma_start(sv, XS[:, :, :]).then_inc(preset, 16)
            for b in range(B):
                sp.wait_ge(rows_sent[b], 16 * NQ)
                for i, (t0, t1) in enumerate(LOADS):
                    t0, t1 = b * NSB + t0, b * NSB + t1
                    sp.dma_start(XS[:, t0:t1], sv[:, t0:t1]).then_inc(slots_in[b][i], 16)

        @block.gpsimd
        def _(pool):
            counts = {}

            def finish(ins, signal):
                counts[signal.name] = counts.get(signal.name, 0) + 1
                ins.then_inc(signal, 1)
                pool.wait_ge(signal, counts[signal.name])

            finish(pool.memset(eps[:, :], EPS), zeroed)
            finish(pool.memset(KG[:, :, 0::2, GK:GP].bitcast(F32), 0.0), zeroed)
            finish(pool.memset(KG[:, :, 1::2, 0:PAD].bitcast(F32), 0.0), zeroed)
            finish(pool.memset(QG[ONES:ONES + 2, 0].bitcast(F32), 1.0), zeroed)
            finish(pool.memset(MR[:, :, :, :, :], 0.0), zeroed)
            finish(pool.memset(MR[:, :, :, :, 0:2], 1.0), zeroed)
            finish(pool.memset(QG[ONES:ONES + 2, 1].bitcast(F32), 1.0), zeroed)
            pool.wait_ge(in_small, 32)
            pool.wait_ge(in_con, 16)
            finish(pool.tensor_scalar(tau8[:, :], TAU[:, :], RS8, None, ALU.mult), tau_ready)
            r = slice(ONES, KR)
            finish(pool.tensor_scalar(dscaled[r, :], DEL[r, :], RS8, None, ALU.mult), erows)
            finish(pool.tensor_copy(dhigh[r, :], dscaled[r, :]), erows)
            finish(pool.tensor_tensor(dlow[r, :], dscaled[r, :], dhigh[r, :].bitcast(F32), ALU.subtract), erows)
            finish(pool.tensor_scalar(dscaled[r, :], dlow[r, :], CON[r, C_SEL + 1:C_SEL + 2], CON[r, C_SEL + 2:C_SEL + 3],
                                      ALU.mult, ALU.subtract), erows)
            finish(pool.tensor_scalar(dlow[r, :], dhigh[r, :].bitcast(F32), CON[r, C_SEL:C_SEL + 1], None, ALU.mult), erows)
            low = dlow[r, :].unsqueeze(1).to_broadcast([KR - ONES, G, B * KEYS])
            rest = dscaled[r, :].unsqueeze(1).to_broadcast([KR - ONES, G, B * KEYS])
            finish(pool.tensor_tensor(Ks[r].rearrange("p g b k -> p g (b k)"), low, rest, ALU.add), erows)
            finish(pool.memset(VP[:, :, :, :, :, HALF * VC:], 0.0), zeroed)
            vm = CON[0:TW, C_VM:C_VM + NT * HALF].rearrange("p (j h) -> p j h", j=NT)
            for l in range(2):
                for b in range(B):
                    for half in range(2):
                        o = VP[:, l, b, :, half, 0:HALF * VC].rearrange("p j (h c) -> p j h c", c=VC)[:, :, :, DK]
                        finish(pool.tensor_copy(o, vm), ones_col)
            pool.wait_ge(in_rows, 16)

            def moe_constants():
                finish(pool.memset(XS[:, :, :], 0.0), blank)
                finish(pool.tensor_copy(XS[:, :, R_ID], CON[:, C_SID:C_SID + NS]), blank)
                tail = CON[:, C_TAIL:C_TAIL + 4 * TILES].rearrange("p (t c) -> p t c", c=4)
                finish(pool.tensor_copy(ROW[:, :, 2 * D:RW], tail), rows_set)
                finish(pool.tensor_copy(trib[:, :], CON[:, C_TRI:C_TRI + 128]), binary)
                finish(pool.memset(onesb[:, :], 1.0), binary)

            for s in steps:
                if s == ("km", 1, 0):
                    moe_constants()
                if s[0] == "km" and s != ("km", 0, 0):
                    _, l, b = s
                    pool.wait_ge(k_split, l + 1)
                    if l == 1:
                        pool.wait_ge(scores_ready, 2 * NT * (b + 1))
                    for odd in (0, 1):
                        finish(pool.tensor_tensor(*masked_k(b, odd), ALU.mult), kg_pool)
                elif s[0] == "xt" and s[1] < 3:
                    _, st, b = s
                    c = (R_BO0, R_WOB, R_BO1)[st]
                    pool.wait_ge(xn_ready, (nth["ln", st, b] + 1) * NQ)
                    row = ROWS[:, c:c + D].unsqueeze(1).to_broadcast([128, NQ, D])
                    finish(pool.tensor_tensor(X[:, b], X[:, b], row, ALU.add), pre_added)
                elif s[0] == "rank":
                    b = s[1]
                    pool.wait_ge(preset, 16)
                    pool.wait_ge(slot_ready, b + 1)
                    pool.wait_ge(b2_ready, b + 1)
                    for i in range(b * NQ, (b + 1) * NQ):
                        pool.indirect_dma_start(slots, bass.IndirectOffsetOnAxis(ap=slot[:, i:i + 1], axis=0), ROW[:, i], None,
                                                bounds_check=NS * 128 - 1, oob_is_err=False).then_inc(rows_sent[b], 16)
                elif s[0] == "moe" and s[1] >= 2:
                    t = s[1] - 2
                    pool.wait_ge(z_ready, t + 1)
                    pool.indirect_dma_start(out, bass.IndirectOffsetOnAxis(ap=token[:, t:t + 1], axis=0), XS[:, t, 0:D], None,
                                            bounds_check=B * S - 1, oob_is_err=False).then_inc(stored, 16)

            pool.wait_ge(stored, 16 * NS)

        @block.scalar
        def _(act):
            act.dma_start(CTX[:, :, :], ctx3).then_inc(in_ctx, 16)
            act.dma_start(CON[:, :], consts).then_inc(in_con, 16)
            act.dma_start(TAU[:, :], tau.partition_broadcast(128)).then_inc(in_small, 16)
            act.preload_act_table_set("natural_log_exp_and_others")
            chain = 0
            act.wait_ge(zeroed, 1)
            for s in steps:
                kind = s[0]
                if kind == "ln":
                    _, st, b = s
                    act.wait_ge(stats_ready, (nth[s] + 1) * NQ)
                    act.activation(logvar[:, b], mean_var[:, b, :, 1], ACT.Ln, bias=eps[:, :]).then_inc(act_chain, 1)
                    chain += 1
                    act.wait_ge(act_chain, chain)
                    act.activation(rstd[:, b], logvar[:, b], ACT.Exp, scale=-0.5).then_inc(rstd_ready, 1)
                elif kind == "xt":
                    _, st, b = s
                    read(act, s)
                    act.activation(XNT[:, b], bank(s)[:, :], ACT.Identity).then_inc(xnt_ready, 1)
                elif kind == "kp":
                    l = s[1]
                    act.wait_ge(in_att[l], 32 if l == 0 else 16)
                    for g in range(G):
                        key = (*s, g // 2)
                        read(act, key)
                        ps = bank(key)[0:QR, (g % 2) * B * KEYS:(g % 2 + 1) * B * KEYS].rearrange("p (b k) -> p b k", b=B)
                        ins = act.activation(Kf[:, g], ps, ACT.Identity, bias=ATT[l][0:QR, A_BK + g:A_BK + g + 1])
                        ins.then_inc(k_biased, 1)
                    act.wait_ge(tau_ready, 1)
                    act.wait_ge(k_biased, G * (l + 1))
                    if l == 1:
                        act.wait_ge(k_split, 1)
                    for b in range(B):
                        act.activation(Kt[:, :, b], Kf[:, :, b], ACT.Identity, scale=tau8[0:QR, b:b + 1]).then_inc(k_scaled, 1)
                elif kind == "q":
                    _, l, b, g = s
                    read(act, s)
                    act.activation(QG[0:QR, b, g], bank(s)[0:QR, :], ACT.Identity,
                                   bias=ATT[l][0:QR, A_BQ + g:A_BQ + g + 1]).then_inc(qh_ready, 1)
                elif kind == "mt":
                    _, l, b, half = s
                    read(act, s)
                    for g in (2 * s[3],):
                        act.activation(QG[ONES:KR, b, g], bank(s)[32 * (g % 2):32 * (g % 2) + KR - ONES, :], ACT.Identity).then_inc(m_act, 1)
                elif kind == "sc":
                    _, l, b, t = s
                    n = (2 * l + b) * 2 * NT + t
                    w = WIDTHS[t % NT]
                    act.wait_ge(scores_ready, n + 1)
                    if n >= NP:
                        act.wait_ge(probs_used, n - NP + 1)
                    act.activation(P[0:w, n % NP], scores[n % 2][0:w, :], ACT.Exp).then_inc(probs_ready, 1)
                elif kind == "ot":
                    _, l, b = s
                    read(act, s)
                    act.activation(OT[:, b], bank(s)[:, :], ACT.Identity, bias=ATT[l][:, A_BV:A_BV + 1]).then_inc(ot_ready, 1)
                elif kind == "hid":
                    _, b, k = s
                    if k % 2 == 0:
                        read(act, s)
                        act.activation(HT[:, b, k], bank(s)[:, :], ACT.Relu,
                                       bias=W0[:, W_WIB + k:W_WIB + k + 1]).then_inc(hid_act, 1)
                elif kind == "route":
                    b = s[1]
                    act.wait_ge(lg_ready, b + 1)
                    act.activation(ex[:, b], lg[:, b], ACT.Exp).then_inc(ex_ready, 1)
                elif kind == "ct":
                    b = s[1]
                    read(act, s)
                    act.activation(CT[:, b], bank(s)[0:E, :], ACT.Identity).then_inc(ct_ready, 1)
                elif kind == "moe":
                    t = s[1]
                    if t + 1 < NS:
                        n = t + 1
                        act.wait_ge(xst_full, n + 1)
                        act.activation(XST[:, n % 2], xst_ps(n), ACT.Identity).then_inc(xst_ready, 1)
                    if 0 <= t < NS:
                        act.wait_ge(biased, t + 1)
                        if t >= NHB:
                            act.wait_ge(y_full, t - NHB + 1)
                        act.activation(HG1[:, t % NHB], HB[:, t % 2], ACT.Gelu_apprx_tanh).then_inc(gelu_ready, 1)

        @block.vector
        def _(dve):
            chain = [0]

            def link(ins):
                chain[0] += 1
                ins.then_inc(dve_chain, 1)
                dve.wait_ge(dve_chain, chain[0])

            expert = {}
            for s in steps:
                kind = s[0]
                if kind == "ln":
                    _, st, b = s
                    if st == 0:
                        dve.wait_ge(in_x[b], 16)
                    for t in range(NQ):
                        ins = dve.bn_stats(stats[:, b, t], X[:, b, t])
                    link(ins)
                    for t in range(NQ):
                        dve.bn_aggr(mean_var[:, b, t], stats[:, b, t]).then_inc(stats_ready, 1)
                    dve.wait_ge(stats_ready, (nth[s] + 1) * NQ)
                    dve.wait_ge(rstd_ready, nth[s] + 1)
                    for t in range(NQ):
                        xn = ROW[:, b * NQ + t, D:2 * D] if st == 3 else XN[:, b, t]
                        dve.tensor_scalar(xn, X[:, b, t], mean_var[:, b, t, 0:1], rstd[:, b, t:t + 1],
                                          ALU.subtract, ALU.mult).then_inc(xn_ready, 1)
                elif kind == "kp":
                    l = s[1]
                    dve.wait_ge(k_scaled, B * (l + 1))
                    if l == 1:
                        dve.wait_ge(kg_dve, 2)
                        dve.wait_ge(kg_pool, 2)
                    link(dve.tensor_copy(Ks[0:QR], Kt[:, :, :, :]))
                    dve.tensor_tensor(Ks[32:64], Kt[32:64], Ks[32:64].bitcast(F32), ALU.subtract).then_inc(k_split, 1)
                elif s == ("km", 0, 0):
                    b = s[2]
                    dve.wait_ge(k_split, 1)
                    dve.wait_ge(erows, 6)
                    for odd in (0, 1):
                        dve.tensor_tensor(*masked_k(b, odd), ALU.mult).then_inc(kg_dve, 1)
                elif kind == "vp":
                    _, l, b, j = s
                    read(dve, s)
                    if (l, b, j) == (0, 0, 0):
                        dve.wait_ge(in_con, 16)
                    w = WIDTHS[j]
                    o = VP[0:w, l, b, j, :, 0:HALF * VC].rearrange("p s (h c) -> p s h c", c=VC)[:, :, :, 0:DK]
                    v = bank(s)[0:w, 0:D].rearrange("p (s h c) -> p s h c", s=2, c=DK)
                    m = CON[0:w, C_VM + HALF * j:C_VM + HALF * (j + 1)].unsqueeze(1).unsqueeze(3).to_broadcast([w, 2, HALF, DK])
                    dve.tensor_tensor(o, v, m, ALU.mult).then_inc(v_ready, 1)
                elif kind == "q":
                    _, l, b, g = s
                    dve.wait_ge(qh_ready, nth[s] + 1)
                    dve.scalar_tensor_tensor(QG[64:96, b, g], bank(s)[64:96, :], ATT[l][64:96, A_BQ + g:A_BQ + g + 1],
                                             QG[64:96, b, g].bitcast(F32), ALU.add, ALU.subtract).then_inc(ql_ready, 1)
                elif kind == "max":
                    _, l, b, i = s
                    n = (2 * l + b) * NQ * G + i
                    g, qt = divmod(i, NQ)
                    if n == 0:
                        dve.wait_ge(zeroed, 5)
                    dve.wait_ge(max_full, n + 1)
                    dve.tensor_reduce(MR[:, b, qt, g, 2:2 + HG],
                                      maxps[n % 2][:, 0:GK].rearrange("p (h k) -> p h k", h=HG),
                                      AX.X, ALU.max).then_inc(max_read, 1)
                elif kind == "mt":
                    _, l, b, half = s
                    read(dve, s)
                    for g in (2 * half + 1,):
                        dve.tensor_copy(QG[ONES:KR, b, g], bank(s)[32 * (g % 2):32 * (g % 2) + KR - ONES, :]).then_inc(m_dve, 1)
                elif kind == "on":
                    _, l, b = s
                    n = 2 * l + b
                    dve.wait_ge(probs_used, 2 * NT * (n + 1))
                    for i in range(2):
                        o = acc[i][:, 0:4 * HALF * VC].rearrange("p (t h c) -> p t h c", t=2, c=VC)
                        ins = dve.reciprocal(rden[:, b, 2 * i:2 * i + 2], o[:, :, :, DK])
                    link(ins)
                    for i in range(2):
                        o = acc[i][:, 0:4 * HALF * VC].rearrange("p (t h c) -> p t h c", t=2, c=VC)
                        rd = rden[:, b, 2 * i:2 * i + 2].unsqueeze(3).to_broadcast([128, 2, H, DK])
                        dve.tensor_tensor(ON[:, b, 2 * i:2 * i + 2].rearrange("p t (h c) -> p t h c", c=DK),
                                          o[:, :, :, 0:DK], rd, ALU.mult).then_inc(on_ready, 1)
                elif kind == "b2":
                    b = s[1]
                    read(dve, s)
                    dve.tensor_tensor(ROW[:, b * NQ:(b + 1) * NQ, 0:D], X[:, b], bank(s)[:, :].rearrange("p (t d) -> p t d", t=NQ),
                                      ALU.add).then_inc(b2_ready, 1)
                elif kind in ("wo", "out"):
                    b = s[-1]
                    st = 1 if kind == "out" else 2 * s[1]
                    dve.wait_ge(pre_added, nth["pre", st, b] + 1)
                    read(dve, s)
                    dve.tensor_tensor(X[:, b], X[:, b], bank(s)[:, :].rearrange("p (t d) -> p t d", t=NQ),
                                      ALU.add).then_inc(x_ready, 1)
                    dve.wait_ge(x_ready, nth[s] + 1)
                elif kind in ("gate", "route"):
                    b = s[1]
                    width = E + E * R if kind == "gate" else E
                    c = R_GB if kind == "gate" else R_SB
                    read(dve, s)
                    ps = bank(s)[:, 0:NQ * width].rearrange("p (t e) -> p t e", t=NQ)
                    gb = ROWS[:, c:c + E].unsqueeze(1).to_broadcast([128, NQ, E])
                    link(dve.tensor_tensor(lg[:, b], ps[:, :, 0:E], gb, ALU.add))
                    link(dve.tensor_reduce(lmax[:, b], lg[:, b], AX.X, ALU.max))
                    mb = lmax[:, b].unsqueeze(2).to_broadcast([128, NQ, E])
                    link(dve.tensor_tensor(eq[:, b], lg[:, b], mb, ALU.is_equal))
                    if kind == "route":
                        dve.tensor_tensor(lg[:, b], lg[:, b], mb, ALU.subtract).then_inc(lg_ready, 1)
                    ew = CON[:, C_EW:C_EW + E].unsqueeze(1).to_broadcast([128, NQ, E])
                    link(dve.tensor_tensor(eq[:, b], eq[:, b], ew, ALU.mult))
                    link(dve.tensor_reduce(first[:, b], eq[:, b], AX.X, ALU.max))
                    fb = first[:, b].unsqueeze(2).to_broadcast([128, NQ, E])
                    link(dve.tensor_tensor(hot[:, b], eq[:, b], fb, ALU.is_equal))
                    if kind == "route":
                        dve.tensor_copy(hotb[:, b * NQ:(b + 1) * NQ], hot[:, b]).then_inc(hot_ready, 1)
                    if kind == "gate":
                        for i in range(3):
                            o = U3[:, b, :, 32 * i:32 * i + 32].rearrange("p t (e r) -> p t e r", r=R)
                            u = ps[:, :, E:].rearrange("p t (e r) -> p t e r", r=R)
                            hb = hot[:, b].unsqueeze(3).to_broadcast([128, NQ, E, R])
                            dve.tensor_tensor(o, u, hb, ALU.mult).then_inc(u3_ready, 1)
                    else:
                        dve.wait_ge(ex_ready, b + 1)
                        link(dve.tensor_reduce(esum[:, b], ex[:, b], AX.X, ALU.add))
                        link(dve.reciprocal(esum[:, b], esum[:, b]))
                        pb = esum[:, b].unsqueeze(2).to_broadcast([128, NQ, E])
                        dve.tensor_tensor(coef[:, b], hot[:, b], pb, ALU.mult).then_inc(coef_ready, 1)
                        dve.wait_ge(rows_set, 1)
                        dve.tensor_copy(ROW[:, b * NQ:(b + 1) * NQ, R_P], esum[:, b])
                elif kind == "ut":
                    b = s[1]
                    if b == 0:
                        dve.wait_ge(in_lb, 48)
                        link(dve.tensor_copy(LS[:, :], LB[0:QR, :]))
                        dve.tensor_tensor(LS[32:64], LB[32:64], LS[32:64].bitcast(F32), ALU.subtract).then_inc(lb_ready, 1)
                    read(dve, s)
                    link(dve.tensor_copy(U[:, b], bank(s)[0:QR, :]))
                    dve.tensor_tensor(U[64:96, b], bank(s)[64:96, :], U[64:96, b].bitcast(F32), ALU.subtract).then_inc(u_ready, 1)
                elif kind == "hid":
                    _, b, k = s
                    if k % 2 == 1:
                        read(dve, s)
                        dve.tensor_scalar(HT[:, b, k], bank(s)[:, :], W0[:, W_WIB + k:W_WIB + k + 1], 0.0,
                                          ALU.add, ALU.max).then_inc(hid_dve, 1)
                elif kind == "rank":
                    b = s[1]
                    read(dve, s)
                    before_me = bank(s)[:, 0:NQ * E].rearrange("p (t e) -> p t e", e=E)
                    count = bank(s)[:, NQ * E:NQ * E + E]
                    thr = CON[:, C_THR:C_THR + NQ].unsqueeze(1).to_broadcast([128, E, NQ])
                    link(dve.tensor_tensor(above[:, :, :], count.unsqueeze(2).to_broadcast([128, E, NQ]), thr, ALU.is_gt))
                    link(dve.tensor_reduce(tiles_of[:, :], above[:, :, :], AX.X, ALU.add))
                    low = CON[:, C_LOW:C_LOW + E * E].rearrange("p (e f) -> p e f", f=E)
                    link(dve.tensor_tensor(lower[:, :, :], low, tiles_of[:, :].unsqueeze(1).to_broadcast([128, E, E]), ALU.mult))
                    link(dve.tensor_reduce(first_tile[:, :], lower[:, :, :], AX.X, ALU.add))
                    link(dve.scalar_tensor_tensor(place[:, :, :], first_tile[:, :].unsqueeze(1).to_broadcast([128, NQ, E]), 128.0,
                                                  before_me, ALU.mult, ALU.add))
                    link(dve.tensor_tensor(place[:, :, :], place[:, :, :], hot[:, b], ALU.mult))
                    link(dve.tensor_reduce(slot_f[:, :], place[:, :, :], AX.X, ALU.add))
                    dve.tensor_scalar(slot[:, b * NQ:(b + 1) * NQ], slot_f[:, :], float(b * NSB * 128), None,
                                      ALU.add).then_inc(slot_ready, 1)
                    link(dve.tensor_tensor(end_tile[0:1, :], first_tile[0:1, :], tiles_of[0:1, :], ALU.add))
                    no = CON[0:1, C_T:C_T + NSB].unsqueeze(2).to_broadcast([1, NSB, E])
                    link(dve.tensor_tensor(past[:, :, :], no, end_tile[0:1, :].unsqueeze(1).to_broadcast([1, NSB, E]), ALU.is_ge))
                    link(dve.tensor_reduce(tile_f[:, :], past[:, :, :], AX.X, ALU.add))
                    dve.tensor_scalar(tile_e[:, b * NSB:(b + 1) * NSB], tile_f[:, :], float(E - 1), None, ALU.min).then_inc(tile_ready, 1)
                elif kind == "moe":
                    t = s[1]
                    if t == -1:
                        for e in range(E):
                            dve.wait_ge(in_w1[e], 16)
                    if t + 1 < NS:
                        n = t + 1
                        dve.wait_ge(tile_ready, n // NSB + 1)
                        expert[n] = dve.value_load(tile_e[0:1, n:n + 1], min_val=0, max_val=E - 1)
                        if n >= 2:
                            dve.wait_ge(hidden_full, n - 1)
                        dve.tensor_copy(W1C[:, n % 2], W1[:, bass.ds(expert[n] * F, F)]).then_inc(w1_ready, 1)
                    if 0 <= t < NS:
                        dve.wait_ge(hidden_full, t + 1)
                        if t >= 2:
                            dve.wait_ge(gelu_ready, t - 1)
                        bias = B1[:, bass.ds(expert[t] * NF, NF)].unsqueeze(2).to_broadcast([128, NF, 128])
                        dve.tensor_tensor(HB[:, t % 2].rearrange("p (k n) -> p k n", k=NF),
                                          hidden[t % 2][:, :].rearrange("p (k n) -> p k n", k=NF), bias, ALU.add).then_inc(biased, 1)
                    if t - 2 >= 0:
                        n = t - 2
                        for i, (t0, t1) in enumerate(LOADS):
                            if n % NSB == t0:
                                dve.wait_ge(slots_in[n // NSB][i], 16)
                                dve.tensor_copy(token[:, n:n + t1 - t0], XS[:, n:n + t1 - t0, R_ID])
                        dve.wait_ge(y_full, n + 1)
                        dve.scalar_tensor_tensor(XS[:, n, 0:D], acc[n % 2][:, 0:D], XS[:, n, R_P:R_P + 1], XS[:, n, 0:D],
                                                 ALU.mult, ALU.add).then_inc(z_ready, 1)

        @block.tensor
        def _(pe):
            def hold(key):
                if key in before:
                    by = reader(before[key])
                    for signal, value in by if isinstance(by, list) else [by]:
                        pe.wait_ge(signal, value)

            done = full
            expert = {}
            for s in steps:
                kind = s[0]
                if kind == "xt":
                    _, st, b = s
                    if nth[s] == 0:
                        pe.wait_ge(in_con, 16)
                    hold(s)
                    pe.wait_ge(xn_ready, NQ * (nth["ln", st, b] + 1))
                    for t in range(NQ):
                        xn = ROW[:, b * NQ + t, D:2 * D] if st == 3 else XN[:, b, t]
                        ins = pe.transpose(bank(s)[:, 128 * t:128 * t + 128], xn, ident)
                    ins.then_inc(done[use[s][0]], 1)
                elif kind == "kp":
                    l = s[1]
                    pe.wait_ge(in_att[l], 32 if l == 0 else 16)
                    pe.wait_ge(in_ctx, 16)
                    for g in range(G):
                        key = (*s, g // 2)
                        if g % 2 == 0:
                            hold(key)
                        ins = pe.matmul(bank(key)[0:QR, (g % 2) * B * KEYS:(g % 2 + 1) * B * KEYS].rearrange("p (b k) -> p b k", b=B),
                                        ATT[l][:, A_K + QR * g:A_K + QR * (g + 1)], CTX[:, :, 0:KEYS], start=True, stop=True)
                        if g % 2 == 1:
                            ins.then_inc(done[use[key][0]], 1)
                elif kind == "vp":
                    _, l, b, j = s
                    if (b, j) == (0, 0):
                        pe.wait_ge(in_att[l], 32 if l == 0 else 16)
                        pe.wait_ge(in_ctx, 16)
                    hold(s)
                    w, k0 = WIDTHS[j], STARTS[j] % KEYS
                    pe.matmul(bank(s)[0:w, 0:D], CTX[:, b, k0:k0 + w], ATT[l][:, A_V:A_V + D],
                              start=True, stop=True).then_inc(done[use[s][0]], 1)
                elif kind == "q":
                    _, l, b, g = s
                    pe.wait_ge(xnt_ready, nth["xt", 2 * l, b] + 1)
                    hold(s)
                    pe.matmul(bank(s)[0:QR, :], ATT[l][:, A_Q + QR * g:A_Q + QR * (g + 1)], XNT[:, b], start=True,
                              stop=True).then_inc(done[use[s][0]], 1)
                elif kind == "max":
                    _, l, b, i = s
                    n = nth[s]
                    g, qt = divmod(i, NQ)
                    if qt == 0:
                        pe.wait_ge(ql_ready, nth["q", l, b, g] + 1)
                        if (l, b) == (0, 0):
                            pe.wait_ge(kg_dve, min(g, 1) + 1)
                        else:
                            pe.wait_ge(kg_pool, 2 * (2 * l + b - 1) + min(g, 1) + 1)
                    if i == 0:
                        pe.wait_ge(zeroed, (4, 7)[b])
                    if n >= 2:
                        pe.wait_ge(max_read, n - 1)
                    off = PAD * (g % 2)
                    pe.matmul(maxps[n % 2][:, 0:GK], QG[0:ONES + 2, b, g, 128 * qt:128 * qt + 128],
                              KG[0:ONES + 2, b, g, off:off + GK], start=True, stop=True).then_inc(max_full, 1)
                elif kind == "mt":
                    _, l, b, half = s
                    hold(s)
                    pe.wait_ge(max_read, nth["max", l, b, 2 * NQ * (half + 1) - 1] + 1)
                    pe.wait_ge(zeroed, 6)
                    for t in range(NQ):
                        m = MR[:, b, t, 2 * half:2 * half + 2].rearrange("p g c -> p (g c)")
                        ins = pe.transpose(bank(s)[0:64, 128 * t:128 * t + 128], m, ident)
                    ins.then_inc(done[use[s][0]], 1)
                elif kind == "sc":
                    _, l, b, t = s
                    n = nth[s]
                    half, j = divmod(t, NT)
                    w = WIDTHS[j]
                    if j == 0:
                        pe.wait_ge(m_act, nth["mt", l, b, half] + 1)
                        pe.wait_ge(m_dve, nth["mt", l, b, half] + 1)
                    if n >= 2:
                        pe.wait_ge(probs_ready, n - 1)
                    parts = {0: [(0, 0)], 1: [(0, 123)], 2: [(0, 246), (1, 0)], 3: [(1, 124)], 4: [(1, 247)]}[j]
                    for i, (odd, c) in enumerate(parts):
                        g = 2 * half + odd
                        ins = pe.matmul(scores[n % 2][0:w, :], KG[:, b, g, c:c + w], QG[:, b, g],
                                        start=(i == 0), stop=(i == len(parts) - 1))
                    ins.then_inc(scores_ready, 1)
                elif kind == "pv":
                    _, l, b, t = s
                    n = nth[s]
                    half, j = divmod(t, NT)
                    w = WIDTHS[j]
                    if t == 0:
                        pe.wait_ge(v_ready, NT * (B * l + b + 1))
                        pe.wait_ge(zeroed, 8)
                        pe.wait_ge(ones_col, 2 * (B * l + b + 1))
                        if n > 0:
                            pe.wait_ge(on_ready, 2 * nth["on", l, b])
                    pe.wait_ge(probs_ready, n + 1)
                    cols = HALF * VC
                    for qt in range(NQ):
                        c = (qt % 2) * 2 * cols + half * cols
                        ins = pe.matmul(acc[qt // 2][:, c:c + VW], P[0:w, n % NP, 128 * qt:128 * qt + 128],
                                        VP[0:w, l, b, j, half],
                                        start=(t == 0 and qt % 2 == 0), stop=(t == 2 * NT - 1 and qt % 2 == 1),
                                        skip_group_check=True)
                    ins.then_inc(probs_used, 1)
                elif kind == "ot":
                    _, l, b = s
                    hold(s)
                    pe.wait_ge(on_ready, 2 * (nth["on", l, b] + 1))
                    for t in range(NQ):
                        ins = pe.transpose(bank(s)[:, 128 * t:128 * t + 128], ON[:, b, t], ident)
                    ins.then_inc(done[use[s][0]], 1)
                elif kind == "wo":
                    _, l, b = s
                    hold(s)
                    pe.wait_ge(ot_ready, nth["ot", l, b] + 1)
                    for t in range(NQ):
                        ins = pe.matmul(bank(s)[:, D * t:D * (t + 1)], OT[:, b, 128 * t:128 * t + 128],
                                        ATT[l][:, A_O:A_O + D], start=True, stop=True)
                    ins.then_inc(done[use[s][0]], 1)
                elif kind in ("gate", "route"):
                    b = s[1]
                    st = 1 if kind == "gate" else 3
                    width = E + E * R if kind == "gate" else E
                    w = W0[:, W_GA:W_GA + width] if kind == "gate" else SW[:, :]
                    if b == 0:
                        pe.wait_ge(*((in_w0, 16) if kind == "gate" else (in_moe, 48)))
                    hold(s)
                    pe.wait_ge(xnt_ready, nth["xt", st, b] + 1)
                    for t in range(NQ):
                        ins = pe.matmul(bank(s)[:, width * t:width * (t + 1)], XNT[:, b, 128 * t:128 * t + 128], w,
                                        start=True, stop=True)
                    ins.then_inc(done[use[s][0]], 1)
                elif kind == "ut":
                    b = s[1]
                    hold(s)
                    pe.wait_ge(u3_ready, 3 * (nth[s] + 1))
                    for t in range(NQ):
                        ins = pe.transpose(bank(s)[0:QR, 128 * t:128 * t + 128], U3[:, b, t], ident)
                    ins.then_inc(done[use[s][0]], 1)
                elif kind == "hid":
                    _, b, k = s
                    hold(s)
                    pe.matmul(bank(s)[:, :], W0[:, W_WI + 128 * k:W_WI + 128 * (k + 1)], XNT[:, b], start=True, stop=False)
                    if k == 0:
                        pe.wait_ge(u_ready, nth["ut", b] + 1)
                        pe.wait_ge(lb_ready, 1)
                    pe.matmul(bank(s)[:, :], LS[:, 128 * k:128 * (k + 1)], U[:, b], start=False,
                              stop=True).then_inc(done[use[s][0]], 1)
                elif kind == "out":
                    b = s[-1]
                    hold(s)
                    pe.wait_ge(hid_act, 2 * (b + 1))
                    pe.wait_ge(hid_dve, 2 * (b + 1))
                    for t in range(NQ):
                        for k in range(NF):
                            w = W0[:, W_WO + D * k:W_WO + D * (k + 1)]
                            ins = pe.matmul(bank(s)[:, D * t:D * (t + 1)], HT[:, b, k, 128 * t:128 * t + 128], w,
                                            start=(k == 0), stop=(k == NF - 1))
                    ins.then_inc(done[use[s][0]], 1)
                elif kind == "ct":
                    b = s[1]
                    hold(s)
                    pe.wait_ge(coef_ready, b + 1)
                    for t in range(NQ):
                        ins = pe.transpose(bank(s)[0:E, 128 * t:128 * t + 128], coef[:, b, t], ident)
                    ins.then_inc(done[use[s][0]], 1)
                elif kind == "b2":
                    b = s[1]
                    hold(s)
                    pe.wait_ge(ct_ready, b + 1)
                    for t in range(NQ):
                        ins = pe.matmul(bank(s)[:, D * t:D * (t + 1)], CT[:, b, 128 * t:128 * t + 128], B2[:, :],
                                        start=True, stop=True)
                    ins.then_inc(done[use[s][0]], 1)
                elif kind == "rank":
                    b = s[1]
                    hold(s)
                    pe.wait_ge(hot_ready, b + 1)
                    pe.wait_ge(binary, 2)
                    ps = bank(s)
                    pe.matmul(ps[:, 0:NQ * E], trib[:, :], hotb[:, b * NQ:(b + 1) * NQ, :].rearrange("p t e -> p (t e)"),
                              start=True, stop=False, skip_group_check=True)
                    for i in range(NQ):
                        n = NQ - i
                        ins = pe.matmul(ps[:, E * (i + 1):E * (NQ + 1)].rearrange("p (t e) -> p t e", e=E), onesb[:, :],
                                        hotb[:, b * NQ + i].unsqueeze(1).to_broadcast([128, n, E]), start=False, stop=(i == NQ - 1),
                                        skip_group_check=True)
                    ins.then_inc(done[use[s][0]], 1)
                elif kind == "moe":
                    t = s[1]
                    if t == -1:
                        for e in range(E):
                            pe.wait_ge(in_w2[e], 16)
                        pe.wait_ge(max_read, 2 * B * NQ * G)
                        pe.wait_ge(probs_ready, 2 * B * 2 * NT)
                    if t + 1 < NS:
                        n = t + 1
                        pe.wait_ge(tile_ready, n // NSB + 1)
                        expert[n] = pe.value_load(tile_e[0:1, n:n + 1], min_val=0, max_val=E - 1)
                        for i, (t0, t1) in enumerate(LOADS):
                            if n % NSB == t0:
                                pe.wait_ge(slots_in[n // NSB][i], 16)
                        if n >= 2:
                            pe.wait_ge(xst_ready, n - 1)
                        pe.transpose(xst_ps(n), XS[:, n, D:2 * D], ident).then_inc(xst_full, 1)
                    if 0 <= t < NS:
                        pe.wait_ge(xst_ready, t + 1)
                        pe.wait_ge(w1_ready, t + 1)
                        if t >= 2:
                            pe.wait_ge(biased, t - 1)
                        for k in range(NF):
                            ins = pe.matmul(hidden[t % 2][:, 128 * k:128 * (k + 1)], W1C[:, t % 2, 128 * k:128 * (k + 1)],
                                            XST[:, t % 2], start=True, stop=True)
                        ins.then_inc(hidden_full, 1)
                    if t >= 2:
                        n = t - 2
                        pe.wait_ge(gelu_ready, n + 1)
                        if n == 0:
                            pe.wait_ge(on_ready, 2 * 2 * B)
                        if n >= 2:
                            pe.wait_ge(z_ready, n - 1)
                        for k in range(NF):
                            ins = pe.matmul(acc[n % 2][:, 0:D], HG1[:, n % NHB, 128 * k:128 * (k + 1)],
                                            W2[:, bass.ds(expert[n] * (NF * D) + D * k, D)], start=(k == 0), stop=(k == NF - 1))
                        ins.then_inc(y_full, 1)


_INS = ["x", "ctx3", "att0", "att1", "consts", "rows", "delta", "tau", "ffn0w", "loraB", "sw", "w1", "b1", "w2", "b2"]


def constants():
    c = np.zeros((128, C_N), np.float32)
    c[:, C_ID:C_ID + 128] = np.eye(128)
    for j in range(NT):
        for r in range(WIDTHS[j]):
            c[r, C_VM + HALF * j + (STARTS[j] + r) // KEYS] = 1
    for r in range(QR):
        c[r, C_KM + (r % 32) // DK] = 1
    c[ONES:ONES + 2, C_KM:C_KM + HG] = 1
    c[:, C_EW:C_EW + E] = np.arange(E, 0, -1)
    c[ONES, C_SEL] = 1
    c[ONES + 1, C_SEL + 1] = 1
    for h in range(HG):
        c[ONES + 2 + h, C_KM + h] = 1
        c[ONES + 2 + h, C_SEL + 2] = 1
    p = np.arange(128)
    for t in range(TILES):
        c[:, C_TAIL + 4 * t + 1] = 128 * t + p
    for t in range(NS):
        c[:, C_SID + t] = B * S + 128 * t + p
    c[:, C_T:C_T + NSB] = np.arange(NSB)
    c[:, C_THR:C_THR + NQ] = 128 * np.arange(NQ)
    c[:, C_LOW:C_LOW + E * E] = np.tri(E, E, -1).reshape(-1)
    c[:, C_TRI:C_TRI + 128] = np.tri(128, 128, -1).T
    return c


def kernel(**inputs):
    import concourse.bacc as _bacc
    from concourse.bass_utils import run_bass_kernel_spmd as _run

    a = {k: np.asarray(v) for k, v in inputs.items()}

    def attention_weights(l):
        p = f"L{l}_xcond_"
        out = np.zeros((128, A_N), np.float32)
        for g in range(G):
            for i in range(3):
                rows_ = slice(32 * g, 32 * g + 32)
                for c, cb, n in ((A_K, A_BK, "k"), (A_Q, A_BQ, "q")):
                    out[:, c + QR * g + 32 * i:c + QR * g + 32 * (i + 1)] = a[p + "W" + n][rows_].T
                    out[32 * i:32 * (i + 1), cb + g] = a[p + "b" + n][rows_]
        out[:, A_V:A_V + D] = a[p + "Wv"].T
        out[:, A_O:A_O + D] = a[p + "Wo"].T
        out[:, A_BV] = a[p + "bv"]
        return out

    ctx_t = a["ctx_1024"].transpose(2, 0, 1)
    f0 = "L0_ffn_"
    by_tile = lambda w: w.reshape(NF, 128, -1).transpose(1, 0, 2).reshape(128, -1)
    arrays = {
        "x": a["x"].reshape(B * S, D),
        "ctx3": np.concatenate([ctx_t] * 3, axis=2),
        "att0": attention_weights(0),
        "att1": attention_weights(1),
        "consts": constants(),
        "rows": np.concatenate([a["L0_xcond_bo"], a[f0 + "wo_b"], a["L1_xcond_bo"], a[f0 + "gate_b"], a["L1_ffn_switch_b"]]),
        "delta": a["fside_BxS2_0"].reshape(-1),
        "tau": a["condB_tau"],
        "ffn0w": np.concatenate([a[f0 + "gate_W"].T, a[f0 + "lora_A"].reshape(E * R, D).T, a[f0 + "wi_W"].T,
                                 by_tile(a[f0 + "wo_W"].T), a[f0 + "wi_b"].reshape(NF, 128).T], axis=1),
        "loraB": a[f0 + "lora_B"].transpose(0, 2, 1).reshape(E * R, F),
        "sw": a["L1_ffn_switch_w"],
        "w1": a["L1_ffn_w1"].transpose(1, 0, 2),
        "b1": a["L1_ffn_b1"].reshape(E, NF, 128).transpose(2, 0, 1).reshape(128, E * NF),
        "w2": a["L1_ffn_w2"].reshape(E, NF, 128, D).transpose(2, 0, 1, 3).reshape(128, E, NF * D),
        "b2": a["L1_ffn_b2"],
    }
    nc = _bacc.Bacc("TRN2", target_bir_lowering=False, num_devices=1)
    feeds, args = {}, []
    for name in _INS:
        v = np.ascontiguousarray(arrays[name])
        feeds[f"in_{name}"] = v
        args.append(nc.dram_tensor(f"in_{name}", v.shape, mybir.dt.from_np(v.dtype), kind="ExternalInput").ap())
    out = nc.dram_tensor("out", (B * S, D), F32, kind="ExternalOutput").ap()
    build(nc, *args, out)
    r = _run(nc, [feeds], core_ids=[0])
    return r.results[0]["out"].reshape(B, S, D)
```

```python
from contextlib import ExitStack

import numpy as np
import concourse.bass as bass
from concourse import mybir

F32 = mybir.dt.float32
F32R = mybir.dt.float32r
BF16 = mybir.dt.bfloat16
I32 = mybir.dt.int32
ALU = mybir.AluOpType
ACT = mybir.ActivationFunctionType
AX = mybir.AxisListType

B = 2
S = 512
D = 128
NQ = S // 128
KEYS = 77
H = 16
DK = D // H
G = 4
HG = H // G
GK = HG * KEYS
HALF = 8
NT = 5
STARTS = [0, 123, 246, 370, 493]
WIDTHS = [123, 123, 124, 123, 123]
TW = 124
GP = 370
PAD = GP - GK
QR = 3 * 32
ONES = QR
KR = QR + 2 + HG
VC = DK + 1
VW = 128
E = 8
R = 4
F = 512
NF = F // 128
EPS = 1e-5
TILES = B * NQ
NSB = NQ + E - 1
NS = B * NSB
RW = 2 * D + 4
R_P, R_ID = 2 * D, 2 * D + 1
LOADS = [(0, 1), (1, 3), (3, 6), (6, NSB)]
NBANK = 4
NHB = 3
RS8 = 1.0 / float(np.sqrt(np.float32(DK)))

A_K, A_Q, A_V, A_O = 0, G * QR, 2 * G * QR, 2 * G * QR + D
A_BK = A_O + D
A_BQ = A_BK + G
A_BV = A_BQ + G
A_N = A_BV + 1
C_ID = 0
C_VM = C_ID + 128
C_KM = C_VM + NT * HALF
C_EW = C_KM + HG
C_SEL = C_EW + E
C_TAIL = C_SEL + 3
C_SID = C_TAIL + 4 * TILES
C_THR = C_SID + NS
C_LOW = C_THR + NQ
C_T = C_LOW + E * E
C_TRI = C_T + NSB
C_N = C_TRI + 128
R_BO0, R_WOB, R_BO1, R_GB, R_SB = 0, D, 2 * D, 3 * D, 3 * D + E
R_N = R_SB + E
W_GA, W_WI, W_WO = 0, E + E * R, E + E * R + F
W_WIB = W_WO + NF * D
W_N = W_WIB + NF


def schedule():
    table = """
        ln/0/0 ln/0/1 xt/0/0 kp/0 delta q/0/0/0:4 km/0/0 max/0/0/0:5 vp/0/0/0:2 max/0/0/5:7 km/0/1 max/0/0/7:9
        vp/0/0/2 max/0/0/9 mt/0/0/0 vp/0/0/3:5 sc/0/0/0 vp/0/1/0 sc/0/0/1 max/0/0/10:12 xt/0/1 max/0/0/12 pv/0/0/0
        max/0/0/13 sc/0/0/2 pv/0/0/1 sc/0/0/3 pv/0/0/2 sc/0/0/4 max/0/0/14:16 mt/0/0/1 vp/0/1/1 q/0/1/0 pv/0/0/3
        vp/0/1/2 q/0/1/1 sc/0/0/5 max/0/1/0 q/0/1/2 vp/0/1/3 pv/0/0/4 max/0/1/1 sc/0/0/6 pv/0/0/5:7 sc/0/0/7 q/0/1/3
        sc/0/0/8 vp/0/1/4 max/0/1/2 pv/0/0/7 max/0/1/3:8 sc/0/0/9 max/0/1/8 pv/0/0/8:10 on/0/0 mt/0/1/0 max/0/1/9
        ot/0/0 max/0/1/10 sc/0/1/0:2 max/0/1/11 wo/0/0 pv/0/1/0 max/0/1/12:14 sc/0/1/2 ln/1/0 max/0/1/14 pv/0/1/1 kp/1
        max/0/1/15 vp/1/0/0 xt/1/0 sc/0/1/3 pv/0/1/2 gate/0 mt/0/1/1 sc/0/1/4 vp/1/0/1 pv/0/1/3:5 sc/0/1/5 ut/0
        pv/0/1/5 hid/0/0:3 sc/0/1/6 hid/0/3 vp/1/0/2 sc/0/1/7 km/1/0 vp/1/0/3:5 pv/0/1/6 vp/1/1/0 sc/0/1/8 pv/0/1/7
        sc/0/1/9 vp/1/1/1:3 out/0 ln/2/0 pv/0/1/8:10 on/0/1 xt/2/0 q/1/0/0:2 vp/1/1/3 max/1/0/0:4 vp/1/1/4 q/1/0/2
        max/1/0/4 ot/0/1 max/1/0/5 wo/0/1 max/1/0/6:8 ln/1/1 km/1/1 mt/1/0/0 q/1/0/3 xt/1/1 max/1/0/8:12 sc/1/0/0
        gate/1 pv/1/0/0 sc/1/0/1 max/1/0/12:14 sc/1/0/2 max/1/0/14 ut/1 max/1/0/15 pv/1/0/1 sc/1/0/3 hid/1/0:4
        mt/1/0/1 pv/1/0/2 out/1 sc/1/0/4 pv/1/0/3 sc/1/0/5 ln/2/1 pv/1/0/4 sc/1/0/6 pv/1/0/5 sc/1/0/7 xt/2/1 pv/1/0/6
        q/1/1/0:3 sc/1/0/8 max/1/1/0 pv/1/0/7 max/1/1/1:4 sc/1/0/9 max/1/1/4 pv/1/0/8 max/1/1/5:8 pv/1/0/9 on/1/0
        mt/1/1/0 max/1/1/8:10 q/1/1/3 sc/1/1/0 max/1/1/10 ot/1/0 max/1/1/11 sc/1/1/1 pv/1/1/0 max/1/1/12:14 sc/1/1/2
        max/1/1/14 wo/1/0 max/1/1/15 pv/1/1/1 sc/1/1/3 pv/1/1/2 mt/1/1/1 sc/1/1/4 pv/1/1/3 sc/1/1/5 pv/1/1/4:6 ln/3/0
        sc/1/1/6:8 xt/3/0 pv/1/1/6 route/0 pv/1/1/7 sc/1/1/8:10 rank/0 pv/1/1/8:10 on/1/1 ot/1/1 wo/1/1 ln/3/1 moe/-1
        xt/3/1 moe/0 route/1 moe/1 rank/1
    """
    steps = []
    for entry in table.split():
        entry, _, end = entry.partition(":")
        kind, *index = entry.split("/")
        index = [int(i) for i in index]
        steps.append((kind, *index))
        for i in range(index[-1] + 1, int(end)) if end else ():
            steps.append((kind, *index[:-1], i))
    return steps + [("moe", t) for t in range(2, NS + 2)]


def order(steps):
    counts, nth = {}, {}
    for s in steps:
        kind = "x" if s[0] in ("wo", "out") else s[0]
        nth[s] = counts[kind] = counts.get(kind, -1) + 1
        if s[0] == "xt" and s[1] < 3:
            nth["pre", s[1], s[2]] = counts["pre"] = counts.get("pre", -1) + 1
    return nth


def banks(steps):
    uses, times, turn, rotation = {}, [0] * NBANK, 0, NBANK
    for s in steps:
        kind = s[0]
        if kind == "moe":
            rotation = 2
        keys = []
        if kind == "kp":
            keys = [(*s, 0), (*s, 1)]
        elif kind in ("max", "q", "xt", "vp", "mt", "ot", "wo", "gate", "ut", "hid", "out", "route", "rank"):
            keys = [s]
        for k in keys:
            i = turn % rotation
            uses[k] = (i, times[i])
            times[i] += 1
            turn += 1
    return uses


def build(nc, x, ctx3, att0, att1, consts, rows, delta, tau, ffn0w, loraB, sw, w1, b1, w2, b2, out):
    steps = schedule()
    use = banks(steps)
    nth = order(steps)
    before = {}
    for i in range(NBANK):
        mine = [k for k in use if use[k][0] == i]
        before.update(zip(mine[1:], mine))
    stages = ExitStack()
    with stages:
        def sb(name, shape, dt=F32):
            return stages.enter_context(nc.sbuf_tensor(name, shape, dt))

        def sem(name):
            return stages.enter_context(nc.semaphore(name))

        X = sb("X", [128, B, NQ, D])
        CTX = sb("CTX", [128, B, 3 * KEYS])
        ATT = [sb(f"ATT{l}", [128, A_N]) for l in range(2)]
        CON = sb("CON", [128, C_N])
        ROWS = sb("ROWS", [128, R_N])
        DEL = sb("DEL", [128, B * KEYS])
        TAU = sb("TAU", [128, B])
        W0 = sb("W0", [128, W_N])
        LB = sb("LB", [128, F])
        SW = sb("SW", [128, E])
        W1 = sb("W1", [128, E * F])
        B1 = sb("B1", [128, E * NF])
        W2 = sb("W2", [128, E * NF * D])
        B2 = sb("B2", [128, E * D])

        stats = sb("stats", [128, B, NQ, 6])
        mean_var = sb("mean_var", [128, B, NQ, 2])
        logvar = sb("logvar", [128, B, NQ])
        rstd = sb("rstd", [128, B, NQ])
        eps = sb("eps", [128, 1])
        XN = sb("XN", [128, B, NQ, D])
        XNT = sb("XNT", [128, B, S])
        tau8 = sb("tau8", [128, B])
        dscaled = sb("dscaled", [128, B * KEYS])
        dhigh = sb("dhigh", [128, B * KEYS], F32R)
        dlow = sb("dlow", [128, B * KEYS])
        Kf = sb("Kf", [QR, G, B, KEYS])
        Kt = sb("Kt", [QR, G, B, KEYS])
        Ks = sb("Ks", [KR, G, B, KEYS], F32R)
        KG = sb("KG", [KR, B, G, GP], F32R)
        VP = sb("VP", [TW, 2, B, NT, 2, VW])
        QG = sb("QG", [KR, B, G, S], F32R)
        MR = sb("MR", [128, B, NQ, G, 32])
        NP = 3
        P = sb("P", [TW, NP, S])
        rden = sb("rden", [128, B, NQ, H])
        ON = sb("ON", [128, B, NQ, D])
        OT = sb("OT", [128, B, S])
        lg = sb("lg", [128, B, NQ, E])
        lmax = sb("lmax", [128, B, NQ])
        eq = sb("eq", [128, B, NQ, E])
        first = sb("first", [128, B, NQ])
        hot = sb("hot", [128, B, NQ, E])
        U3 = sb("U3", [128, B, NQ, QR])
        U = sb("U", [QR, B, S], F32R)
        LS = sb("LS", [QR, F], F32R)
        HT = sb("HT", [128, B, NF, S])
        ROW = sb("ROW", [128, TILES, RW])
        hotb = sb("hotb", [128, TILES, E], BF16)
        trib = sb("trib", [128, 128], BF16)
        onesb = sb("onesb", [128, 128], BF16)
        above = sb("above", [128, E, NQ])
        tiles_of = sb("tiles_of", [128, E])
        lower = sb("lower", [128, E, E])
        first_tile = sb("first_tile", [128, E])
        end_tile = sb("end_tile", [128, E])
        place = sb("place", [128, NQ, E])
        slot_f = sb("slot_f", [128, NQ])
        slot = sb("slot", [128, TILES], I32)
        past = sb("past", [1, NSB, E])
        tile_f = sb("tile_f", [1, NSB])
        tile_e = sb("tile_e", [1, NS], I32)
        XS = sb("XS", [128, NS, RW])
        XST = sb("XST", [128, 2, 128])
        spare = HT[:, :, :, :].rearrange("p b k n -> p (b k) n")
        W1C, HB, HG1 = spare[:, 0:2], spare[:, 2:4], spare[:, 4:4 + NHB]
        token = sb("token", [128, NS], I32)
        slots = nc.dram_tensor("slots", (NS * 128, RW), F32).ap()
        ex = sb("ex", [128, B, NQ, E])
        esum = sb("esum", [128, B, NQ])
        YB = sb("YB", [128, 2, D])

        scores = [stages.enter_context(nc.psum_tensor(f"scores{i}", [128, 512], F32)) for i in range(2)]
        acc = [stages.enter_context(nc.psum_tensor(f"acc{i}", [128, 512], F32)) for i in range(2)]
        shared = [stages.enter_context(nc.psum_tensor(f"shared{i}", [128, 512], F32)) for i in range(NBANK)]

        in_x = [sem(f"in_x{b}") for b in range(B)]
        in_ctx, in_con, in_small, in_w0, in_lb = sem("in_ctx"), sem("in_con"), sem("in_small"), sem("in_w0"), sem("in_lb")
        in_att = [sem(f"in_att{l}") for l in range(2)]
        in_moe, in_rows = sem("in_moe"), sem("in_rows")
        in_w1 = [sem(f"in_w1_{e}") for e in range(E)]
        in_w2 = [sem(f"in_w2_{e}") for e in range(E)]
        zeroed = sem("zeroed")
        delta_ready = sem("delta_ready")
        ones_col = sem("ones_col")
        pre_added = sem("pre_added")
        k_scaled = sem("k_scaled")
        kg_dve = sem("kg_dve")
        kg_pool = sem("kg_pool")
        full = [sem(f"full{i}") for i in range(NBANK)]
        stats_ready = sem("stats_ready")
        rstd_ready = sem("rstd_ready")
        act_chain = sem("act_chain")
        dve_chain = sem("dve_chain")
        xn_ready = sem("xn_ready")
        xnt_ready = sem("xnt_ready")
        k_biased = sem("k_biased")
        k_split = sem("k_split")
        tau_ready = sem("tau_ready")
        v_ready = sem("v_ready")
        qh_ready = sem("qh_ready")
        ql_ready = sem("ql_ready")
        m_act = sem("m_act")
        m_dve = sem("m_dve")
        max_read = sem("max_read")
        scores_ready = sem("scores_ready")
        probs_ready = sem("probs_ready")
        probs_used = sem("probs_used")
        on_ready = sem("on_ready")
        ot_ready = sem("ot_ready")
        x_ready = sem("x_ready")
        u3_ready = sem("u3_ready")
        u_ready = sem("u_ready")
        lb_ready = sem("lb_ready")
        hid_act = sem("hid_act")
        hid_dve = sem("hid_dve")
        lg_ready = sem("lg_ready")
        ex_ready = sem("ex_ready")
        preset = sem("preset")
        rows_set = sem("rows_set")
        blank = sem("blank")
        hot_ready = sem("hot_ready")
        binary = sem("binary")
        rank_read = sem("rank_read")
        slot_ready = sem("slot_ready")
        tile_ready = sem("tile_ready")
        rows_sent = [sem(f"rows_sent{b}") for b in range(B)]
        slots_in = [[sem(f"slots_in{b}_{i}") for i in range(len(LOADS))] for b in range(B)]
        xst_full = sem("xst_full")
        xst_ready = sem("xst_ready")
        w1_ready = sem("w1_ready")
        hidden_full = sem("hidden_full")
        biased = sem("biased")
        gelu_ready = sem("gelu_ready")
        y_full = sem("y_full")
        z_ready = sem("z_ready")
        token_ready = sem("token_ready")
        stored = sem("stored")

        ident = CON[:, C_ID:C_ID + 128]
        hidden = scores

        def bank(key):
            return shared[use[key][0]]

        def xst_ps(t):
            return shared[2 + t % 2][:, 0:128]

        def masked_k(b, odd):
            off = PAD * odd
            o = KG[:, b, odd::2, off:off + GK].rearrange("p g (h k) -> p g h k", h=HG)
            k4 = Ks[:, odd::2, b].bitcast(F32).unsqueeze(2).to_broadcast([KR, G // 2, HG, KEYS])
            m4 = CON[0:KR, C_KM:C_KM + HG].unsqueeze(1).unsqueeze(3).to_broadcast([KR, G // 2, HG, KEYS])
            return o, k4, m4

        def reader(key):
            kind = key[0]
            if kind == "kp":
                return k_biased, G * key[1] + 2 * (key[2] + 1)
            if kind == "q":
                return ql_ready, nth[key] + 1
            if kind == "mt":
                return [(m_act, nth[key] + 1), (m_dve, nth[key] + 1)]
            if kind == "gate":
                return u3_ready, 3 * (nth[key] + 1)
            if kind == "hid":
                return (hid_dve if key[2] % 2 else hid_act), 2 * key[1] + key[2] // 2 + 1
            by = {"xt": xnt_ready, "vp": v_ready, "ot": ot_ready, "route": lg_ready, "rank": tile_ready,
                  "max": max_read,
                  "ut": u_ready, "wo": x_ready, "out": x_ready}
            return by[kind], nth[key] + 1

        def read(eng, key):
            i, n = use[key]
            eng.wait_ge(full[i], n + 1)

        block = stages.enter_context(nc.Block())

        @block.sync
        def _(sp):
            xv = x.rearrange("(b t p) d -> b p t d", b=B, p=128)
            sp.dma_start(X[:, 0], xv[0]).then_inc(in_x[0], 16)
            sp.dma_start(ATT[0][:, 0:A_Q], att0[:, 0:A_Q]).then_inc(in_att[0], 16)
            sp.dma_start(ATT[0][:, A_Q:], att0[:, A_Q:]).then_inc(in_att[0], 16)
            sp.dma_start(DEL[ONES:KR, :], delta.partition_broadcast(KR - ONES)).then_inc(in_small, 16)
            sp.dma_start(X[:, 1], xv[1]).then_inc(in_x[1], 16)
            sp.dma_start(ROWS[:, :], rows.partition_broadcast(128)).then_inc(in_rows, 16)
            sp.dma_start(W0[:, :], ffn0w).then_inc(in_w0, 16)
            for i in range(3):
                sp.dma_start(LB[32 * i:32 * i + 32, :], loraB).then_inc(in_lb, 16)
            sp.dma_start(ATT[1][:, :], att1).then_inc(in_att[1], 16)
            sp.dma_start(SW[:, :], sw).then_inc(in_moe, 16)
            sp.dma_start(B1[:, :], b1).then_inc(in_moe, 16)
            sp.dma_start(B2[:, :], b2.partition_broadcast(128)).then_inc(in_moe, 16)
            for e in range(E):
                sp.dma_start(W1[:, e * F:(e + 1) * F], w1[:, e]).then_inc(in_w1[e], 16)
                sp.dma_start(W2[:, e * NF * D:(e + 1) * NF * D], w2[:, e]).then_inc(in_w2[e], 16)
            sv = slots.rearrange("(t p) w -> p t w", p=128)
            sp.wait_ge(blank, 2)
            sp.dma_start(sv, XS[:, :, :]).then_inc(preset, 16)
            for b in range(B):
                sp.wait_ge(rows_sent[b], 16 * NQ)
                for i, (t0, t1) in enumerate(LOADS):
                    t0, t1 = b * NSB + t0, b * NSB + t1
                    sp.dma_start(XS[:, t0:t1], sv[:, t0:t1]).then_inc(slots_in[b][i], 16)

        @block.gpsimd
        def _(pool):
            counts = {}

            def finish(ins, signal):
                counts[signal.name] = counts.get(signal.name, 0) + 1
                ins.then_inc(signal, 1)
                pool.wait_ge(signal, counts[signal.name])

            finish(pool.memset(eps[:, :], EPS), zeroed)
            finish(pool.memset(KG[:, :, 0::2, GK:GP].bitcast(F32), 0.0), zeroed)
            finish(pool.memset(KG[:, :, 1::2, 0:PAD].bitcast(F32), 0.0), zeroed)
            finish(pool.memset(QG[ONES:ONES + 2, 0].bitcast(F32), 1.0), zeroed)
            finish(pool.memset(MR[:, :, :, :, :], 0.0), zeroed)
            finish(pool.memset(MR[:, :, :, :, 0:2], 1.0), zeroed)
            finish(pool.memset(QG[ONES:ONES + 2, 1].bitcast(F32), 1.0), zeroed)
            pool.wait_ge(in_small, 32)
            pool.wait_ge(in_con, 16)
            finish(pool.tensor_scalar(tau8[:, :], TAU[:, :], RS8, None, ALU.mult), tau_ready)
            finish(pool.memset(VP[:, :, :, :, :, HALF * VC:], 0.0), zeroed)
            vm = CON[0:TW, C_VM:C_VM + NT * HALF].rearrange("p (j h) -> p j h", j=NT)
            for l in range(2):
                for b in range(B):
                    for half in range(2):
                        o = VP[:, l, b, :, half, 0:HALF * VC].rearrange("p j (h c) -> p j h c", c=VC)[:, :, :, DK]
                        finish(pool.tensor_copy(o, vm), ones_col)
            pool.wait_ge(in_rows, 16)

            def moe_constants():
                finish(pool.memset(XS[:, :, :], 0.0), blank)
                finish(pool.tensor_copy(XS[:, :, R_ID], CON[:, C_SID:C_SID + NS]), blank)
                tail = CON[:, C_TAIL:C_TAIL + 4 * TILES].rearrange("p (t c) -> p t c", c=4)
                finish(pool.tensor_copy(ROW[:, :, 2 * D:RW], tail), rows_set)
                finish(pool.tensor_copy(trib[:, :], CON[:, C_TRI:C_TRI + 128]), binary)
                finish(pool.memset(onesb[:, :], 1.0), binary)

            for s in steps:
                if s == ("km", 1, 0):
                    moe_constants()
                if s[0] == "km" and s != ("km", 0, 0):
                    _, l, b = s
                    pool.wait_ge(k_split, l + 1)
                    pool.wait_ge(delta_ready, 1)
                    if l == 1:
                        pool.wait_ge(scores_ready, 2 * NT * (b + 1))
                    for odd in (0, 1):
                        finish(pool.tensor_tensor(*masked_k(b, odd), ALU.mult), kg_pool)
                elif s[0] == "xt" and s[1] < 3:
                    _, st, b = s
                    c = (R_BO0, R_WOB, R_BO1)[st]
                    pool.wait_ge(xn_ready, (nth["ln", st, b] + 1) * NQ)
                    row = ROWS[:, c:c + D].unsqueeze(1).to_broadcast([128, NQ, D])
                    finish(pool.tensor_tensor(X[:, b], X[:, b], row, ALU.add), pre_added)
                elif s[0] == "rank":
                    b = s[1]
                    pool.wait_ge(preset, 16)
                    pool.wait_ge(slot_ready, b + 1)
                    for i in range(b * NQ, (b + 1) * NQ):
                        pool.indirect_dma_start(slots, bass.IndirectOffsetOnAxis(ap=slot[:, i:i + 1], axis=0), ROW[:, i], None,
                                                bounds_check=NS * 128 - 1, oob_is_err=False).then_inc(rows_sent[b], 16)
                elif s[0] == "moe" and s[1] >= 2:
                    t = s[1] - 2
                    pool.wait_ge(z_ready, t + 1)
                    pool.indirect_dma_start(out, bass.IndirectOffsetOnAxis(ap=token[:, t:t + 1], axis=0), XS[:, t, 0:D], None,
                                            bounds_check=B * S - 1, oob_is_err=False).then_inc(stored, 16)

            pool.wait_ge(stored, 16 * NS)

        @block.scalar
        def _(act):
            act.dma_start(CTX[:, :, :], ctx3).then_inc(in_ctx, 16)
            act.dma_start(CON[:, :], consts).then_inc(in_con, 16)
            act.dma_start(TAU[:, :], tau.partition_broadcast(128)).then_inc(in_small, 16)
            act.preload_act_table_set("natural_log_exp_and_others")
            chain = 0
            act.wait_ge(zeroed, 1)
            for s in steps:
                kind = s[0]
                if kind == "ln":
                    _, st, b = s
                    act.wait_ge(stats_ready, (nth[s] + 1) * NQ)
                    act.activation(logvar[:, b], mean_var[:, b, :, 1], ACT.Ln, bias=eps[:, :]).then_inc(act_chain, 1)
                    chain += 1
                    act.wait_ge(act_chain, chain)
                    act.activation(rstd[:, b], logvar[:, b], ACT.Exp, scale=-0.5).then_inc(rstd_ready, 1)
                elif kind == "xt":
                    _, st, b = s
                    read(act, s)
                    act.activation(XNT[:, b], bank(s)[:, :], ACT.Identity).then_inc(xnt_ready, 1)
                elif kind == "kp":
                    l = s[1]
                    act.wait_ge(in_att[l], 32 if l == 0 else 16)
                    for g in range(G):
                        key = (*s, g // 2)
                        read(act, key)
                        ps = bank(key)[0:QR, (g % 2) * B * KEYS:(g % 2 + 1) * B * KEYS].rearrange("p (b k) -> p b k", b=B)
                        ins = act.activation(Kf[:, g], ps, ACT.Identity, bias=ATT[l][0:QR, A_BK + g:A_BK + g + 1])
                        ins.then_inc(k_biased, 1)
                    act.wait_ge(tau_ready, 1)
                    act.wait_ge(k_biased, G * (l + 1))
                    if l == 1:
                        act.wait_ge(k_split, 1)
                    for b in range(B):
                        act.activation(Kt[:, :, b], Kf[:, :, b], ACT.Identity, scale=tau8[0:QR, b:b + 1]).then_inc(k_scaled, 1)
                elif kind == "q":
                    _, l, b, g = s
                    read(act, s)
                    act.activation(QG[0:QR, b, g], bank(s)[0:QR, :], ACT.Identity,
                                   bias=ATT[l][0:QR, A_BQ + g:A_BQ + g + 1]).then_inc(qh_ready, 1)
                elif kind == "mt":
                    _, l, b, half = s
                    read(act, s)
                    for g in (2 * s[3],):
                        act.activation(QG[ONES:KR, b, g], bank(s)[32 * (g % 2):32 * (g % 2) + KR - ONES, :], ACT.Identity).then_inc(m_act, 1)
                elif kind == "sc":
                    _, l, b, t = s
                    n = (2 * l + b) * 2 * NT + t
                    w = WIDTHS[t % NT]
                    act.wait_ge(scores_ready, n + 1)
                    if n >= NP:
                        act.wait_ge(probs_used, n - NP + 1)
                    act.activation(P[0:w, n % NP], scores[n % 2][0:w, :], ACT.Exp).then_inc(probs_ready, 1)
                elif kind == "ot":
                    _, l, b = s
                    read(act, s)
                    act.activation(OT[:, b], bank(s)[:, :], ACT.Identity, bias=ATT[l][:, A_BV:A_BV + 1]).then_inc(ot_ready, 1)
                elif kind == "hid":
                    _, b, k = s
                    if k % 2 == 0:
                        read(act, s)
                        act.activation(HT[:, b, k], bank(s)[:, :], ACT.Relu,
                                       bias=W0[:, W_WIB + k:W_WIB + k + 1]).then_inc(hid_act, 1)
                elif kind == "route":
                    b = s[1]
                    act.wait_ge(lg_ready, b + 1)
                    act.activation(ex[:, b], lg[:, b], ACT.Exp).then_inc(ex_ready, 1)
                elif kind == "moe":
                    t = s[1]
                    if t == -1:
                        act.wait_ge(x_ready, nth["out", 1] + 1)
                        for e in range(E):
                            act.wait_ge(in_w1[e], 16)
                    if t + 1 < NS:
                        n = t + 1
                        act.wait_ge(tile_ready, n // NSB + 1)
                        expert = act.value_load(tile_e[0:1, n:n + 1], min_val=0, max_val=E - 1)
                        if n >= 2:
                            act.wait_ge(hidden_full, n - 1)
                        act.activation(W1C[:, n % 2], W1[:, bass.ds(expert * F, F)], ACT.Identity).then_inc(w1_ready, 1)
                        act.wait_ge(xst_full, n + 1)
                        act.activation(XST[:, n % 2], xst_ps(n), ACT.Identity).then_inc(xst_ready, 1)
                    if 0 <= t < NS:
                        act.wait_ge(biased, t + 1)
                        if t >= NHB:
                            act.wait_ge(y_full, t - NHB + 1)
                        act.activation(HG1[:, t % NHB], HB[:, t % 2], ACT.Gelu_apprx_tanh).then_inc(gelu_ready, 1)

        @block.vector
        def _(dve):
            chain = [0]

            def link(ins):
                chain[0] += 1
                ins.then_inc(dve_chain, 1)
                dve.wait_ge(dve_chain, chain[0])

            expert = {}
            for s in steps:
                kind = s[0]
                if kind == "ln":
                    _, st, b = s
                    if st == 0:
                        dve.wait_ge(in_x[b], 16)
                    stream = [ROW[:, b * NQ + t, 0:D] if st == 3 else X[:, b, t] for t in range(NQ)]
                    for t in range(NQ):
                        ins = dve.bn_stats(stats[:, b, t], stream[t])
                    link(ins)
                    for t in range(NQ):
                        dve.bn_aggr(mean_var[:, b, t], stats[:, b, t]).then_inc(stats_ready, 1)
                    dve.wait_ge(stats_ready, (nth[s] + 1) * NQ)
                    dve.wait_ge(rstd_ready, nth[s] + 1)
                    for t in range(NQ):
                        xn = ROW[:, b * NQ + t, D:2 * D] if st == 3 else XN[:, b, t]
                        dve.tensor_scalar(xn, stream[t], mean_var[:, b, t, 0:1], rstd[:, b, t:t + 1],
                                          ALU.subtract, ALU.mult).then_inc(xn_ready, 1)
                elif kind == "delta":
                    dve.wait_ge(in_small, 32)
                    dve.wait_ge(in_con, 16)
                    r = slice(ONES, KR)
                    link(dve.tensor_scalar(dscaled[r, :], DEL[r, :], RS8, None, ALU.mult))
                    link(dve.tensor_copy(dhigh[r, :], dscaled[r, :]))
                    link(dve.tensor_tensor(dlow[r, :], dscaled[r, :], dhigh[r, :].bitcast(F32), ALU.subtract))
                    link(dve.tensor_scalar(dscaled[r, :], dlow[r, :], CON[r, C_SEL + 1:C_SEL + 2], CON[r, C_SEL + 2:C_SEL + 3],
                                           ALU.mult, ALU.subtract))
                    link(dve.tensor_scalar(dlow[r, :], dhigh[r, :].bitcast(F32), CON[r, C_SEL:C_SEL + 1], None, ALU.mult))
                    low = dlow[r, :].unsqueeze(1).to_broadcast([KR - ONES, G, B * KEYS])
                    rest = dscaled[r, :].unsqueeze(1).to_broadcast([KR - ONES, G, B * KEYS])
                    dve.tensor_tensor(Ks[r].rearrange("p g b k -> p g (b k)"), low, rest, ALU.add).then_inc(delta_ready, 1)
                elif kind == "kp":
                    l = s[1]
                    dve.wait_ge(k_scaled, B * (l + 1))
                    if l == 1:
                        dve.wait_ge(kg_dve, 2)
                        dve.wait_ge(kg_pool, 2)
                    link(dve.tensor_copy(Ks[0:QR], Kt[:, :, :, :]))
                    dve.tensor_tensor(Ks[32:64], Kt[32:64], Ks[32:64].bitcast(F32), ALU.subtract).then_inc(k_split, 1)
                elif s == ("km", 0, 0):
                    b = s[2]
                    dve.wait_ge(k_split, 1)
                    dve.wait_ge(delta_ready, 1)
                    for odd in (0, 1):
                        dve.tensor_tensor(*masked_k(b, odd), ALU.mult).then_inc(kg_dve, 1)
                elif kind == "vp":
                    _, l, b, j = s
                    read(dve, s)
                    if (l, b, j) == (0, 0, 0):
                        dve.wait_ge(in_con, 16)
                    w = WIDTHS[j]
                    o = VP[0:w, l, b, j, :, 0:HALF * VC].rearrange("p s (h c) -> p s h c", c=VC)[:, :, :, 0:DK]
                    v = bank(s)[0:w, 0:D].rearrange("p (s h c) -> p s h c", s=2, c=DK)
                    m = CON[0:w, C_VM + HALF * j:C_VM + HALF * (j + 1)].unsqueeze(1).unsqueeze(3).to_broadcast([w, 2, HALF, DK])
                    dve.tensor_tensor(o, v, m, ALU.mult).then_inc(v_ready, 1)
                elif kind == "q":
                    _, l, b, g = s
                    dve.wait_ge(qh_ready, nth[s] + 1)
                    dve.scalar_tensor_tensor(QG[64:96, b, g], bank(s)[64:96, :], ATT[l][64:96, A_BQ + g:A_BQ + g + 1],
                                             QG[64:96, b, g].bitcast(F32), ALU.add, ALU.subtract).then_inc(ql_ready, 1)
                elif kind == "max":
                    _, l, b, i = s
                    n = (2 * l + b) * NQ * G + i
                    g, qt = divmod(i, NQ)
                    if n == 0:
                        dve.wait_ge(zeroed, 5)
                    read(dve, s)
                    dve.tensor_reduce(MR[:, b, qt, g, 2:2 + HG],
                                      bank(s)[:, 0:GK].rearrange("p (h k) -> p h k", h=HG),
                                      AX.X, ALU.max).then_inc(max_read, 1)
                elif kind == "mt":
                    _, l, b, half = s
                    read(dve, s)
                    for g in (2 * half + 1,):
                        dve.tensor_copy(QG[ONES:KR, b, g], bank(s)[32 * (g % 2):32 * (g % 2) + KR - ONES, :]).then_inc(m_dve, 1)
                elif kind == "on":
                    _, l, b = s
                    n = 2 * l + b
                    dve.wait_ge(probs_used, 2 * NT * (n + 1))
                    for i in range(2):
                        o = acc[i][:, 0:4 * HALF * VC].rearrange("p (t h c) -> p t h c", t=2, c=VC)
                        ins = dve.reciprocal(rden[:, b, 2 * i:2 * i + 2], o[:, :, :, DK])
                    link(ins)
                    for i in range(2):
                        o = acc[i][:, 0:4 * HALF * VC].rearrange("p (t h c) -> p t h c", t=2, c=VC)
                        rd = rden[:, b, 2 * i:2 * i + 2].unsqueeze(3).to_broadcast([128, 2, H, DK])
                        dve.tensor_tensor(ON[:, b, 2 * i:2 * i + 2].rearrange("p t (h c) -> p t h c", c=DK),
                                          o[:, :, :, 0:DK], rd, ALU.mult).then_inc(on_ready, 1)
                elif kind in ("wo", "out"):
                    b = s[-1]
                    st = 1 if kind == "out" else 2 * s[1]
                    dve.wait_ge(pre_added, nth["pre", st, b] + 1)
                    read(dve, s)
                    o = ROW[:, b * NQ:(b + 1) * NQ, 0:D] if s[:2] == ("wo", 1) else X[:, b]
                    dve.tensor_tensor(o, X[:, b], bank(s)[:, :].rearrange("p (t d) -> p t d", t=NQ),
                                      ALU.add).then_inc(x_ready, 1)
                    dve.wait_ge(x_ready, nth[s] + 1)
                elif kind in ("gate", "route"):
                    b = s[1]
                    width = E + E * R if kind == "gate" else E
                    c = R_GB if kind == "gate" else R_SB
                    read(dve, s)
                    ps = bank(s)[:, 0:NQ * width].rearrange("p (t e) -> p t e", t=NQ)
                    gb = ROWS[:, c:c + E].unsqueeze(1).to_broadcast([128, NQ, E])
                    link(dve.tensor_tensor(lg[:, b], ps[:, :, 0:E], gb, ALU.add))
                    link(dve.tensor_reduce(lmax[:, b], lg[:, b], AX.X, ALU.max))
                    mb = lmax[:, b].unsqueeze(2).to_broadcast([128, NQ, E])
                    link(dve.tensor_tensor(eq[:, b], lg[:, b], mb, ALU.is_equal))
                    if kind == "route":
                        dve.tensor_tensor(lg[:, b], lg[:, b], mb, ALU.subtract).then_inc(lg_ready, 1)
                    ew = CON[:, C_EW:C_EW + E].unsqueeze(1).to_broadcast([128, NQ, E])
                    link(dve.tensor_tensor(eq[:, b], eq[:, b], ew, ALU.mult))
                    link(dve.tensor_reduce(first[:, b], eq[:, b], AX.X, ALU.max))
                    fb = first[:, b].unsqueeze(2).to_broadcast([128, NQ, E])
                    link(dve.tensor_tensor(hot[:, b], eq[:, b], fb, ALU.is_equal))
                    if kind == "route":
                        dve.tensor_copy(hotb[:, b * NQ:(b + 1) * NQ], hot[:, b]).then_inc(hot_ready, 1)
                    if kind == "gate":
                        for i in range(3):
                            o = U3[:, b, :, 32 * i:32 * i + 32].rearrange("p t (e r) -> p t e r", r=R)
                            u = ps[:, :, E:].rearrange("p t (e r) -> p t e r", r=R)
                            hb = hot[:, b].unsqueeze(3).to_broadcast([128, NQ, E, R])
                            dve.tensor_tensor(o, u, hb, ALU.mult).then_inc(u3_ready, 1)
                    else:
                        dve.wait_ge(ex_ready, b + 1)
                        link(dve.tensor_reduce(esum[:, b], ex[:, b], AX.X, ALU.add))
                        link(dve.reciprocal(esum[:, b], esum[:, b]))
                        dve.wait_ge(rows_set, 1)
                        dve.tensor_copy(ROW[:, b * NQ:(b + 1) * NQ, R_P], esum[:, b])
                elif kind == "ut":
                    b = s[1]
                    if b == 0:
                        dve.wait_ge(in_lb, 48)
                        link(dve.tensor_copy(LS[:, :], LB[0:QR, :]))
                        dve.tensor_tensor(LS[32:64], LB[32:64], LS[32:64].bitcast(F32), ALU.subtract).then_inc(lb_ready, 1)
                    read(dve, s)
                    link(dve.tensor_copy(U[:, b], bank(s)[0:QR, :]))
                    dve.tensor_tensor(U[64:96, b], bank(s)[64:96, :], U[64:96, b].bitcast(F32), ALU.subtract).then_inc(u_ready, 1)
                elif kind == "hid":
                    _, b, k = s
                    if k % 2 == 1:
                        read(dve, s)
                        dve.tensor_scalar(HT[:, b, k], bank(s)[:, :], W0[:, W_WIB + k:W_WIB + k + 1], 0.0,
                                          ALU.add, ALU.max).then_inc(hid_dve, 1)
                elif kind == "rank":
                    b = s[1]
                    read(dve, s)
                    before_me = bank(s)[:, 0:NQ * E].rearrange("p (t e) -> p t e", e=E)
                    count = bank(s)[:, NQ * E:NQ * E + E]
                    thr = CON[:, C_THR:C_THR + NQ].unsqueeze(1).to_broadcast([128, E, NQ])
                    link(dve.tensor_tensor(above[:, :, :], count.unsqueeze(2).to_broadcast([128, E, NQ]), thr, ALU.is_gt))
                    link(dve.tensor_reduce(tiles_of[:, :], above[:, :, :], AX.X, ALU.add))
                    low = CON[:, C_LOW:C_LOW + E * E].rearrange("p (e f) -> p e f", f=E)
                    link(dve.tensor_tensor(lower[:, :, :], low, tiles_of[:, :].unsqueeze(1).to_broadcast([128, E, E]), ALU.mult))
                    link(dve.tensor_reduce(first_tile[:, :], lower[:, :, :], AX.X, ALU.add))
                    link(dve.scalar_tensor_tensor(place[:, :, :], first_tile[:, :].unsqueeze(1).to_broadcast([128, NQ, E]), 128.0,
                                                  before_me, ALU.mult, ALU.add))
                    link(dve.tensor_tensor(place[:, :, :], place[:, :, :], hot[:, b], ALU.mult))
                    link(dve.tensor_reduce(slot_f[:, :], place[:, :, :], AX.X, ALU.add))
                    dve.tensor_scalar(slot[:, b * NQ:(b + 1) * NQ], slot_f[:, :], float(b * NSB * 128), None,
                                      ALU.add).then_inc(slot_ready, 1)
                    link(dve.tensor_tensor(end_tile[0:1, :], first_tile[0:1, :], tiles_of[0:1, :], ALU.add))
                    no = CON[0:1, C_T:C_T + NSB].unsqueeze(2).to_broadcast([1, NSB, E])
                    link(dve.tensor_tensor(past[:, :, :], no, end_tile[0:1, :].unsqueeze(1).to_broadcast([1, NSB, E]), ALU.is_ge))
                    link(dve.tensor_reduce(tile_f[:, :], past[:, :, :], AX.X, ALU.add))
                    dve.tensor_scalar(tile_e[:, b * NSB:(b + 1) * NSB], tile_f[:, :], float(E - 1), None, ALU.min).then_inc(tile_ready, 1)
                elif kind == "moe":
                    t = s[1]
                    if t == -1:
                        dve.wait_ge(in_moe, 48)
                    if t + 1 < NS:
                        n = t + 1
                        dve.wait_ge(tile_ready, n // NSB + 1)
                        expert[n] = dve.value_load(tile_e[0:1, n:n + 1], min_val=0, max_val=E - 1)
                    if 0 <= t < NS:
                        dve.wait_ge(hidden_full, t + 1)
                        if t >= 2:
                            dve.wait_ge(gelu_ready, t - 1)
                        bias = B1[:, bass.ds(expert[t] * NF, NF)].unsqueeze(2).to_broadcast([128, NF, 128])
                        dve.tensor_tensor(HB[:, t % 2].rearrange("p (k n) -> p k n", k=NF),
                                          hidden[t % 2][:, :].rearrange("p (k n) -> p k n", k=NF), bias, ALU.add).then_inc(biased, 1)
                    if t - 2 >= 0:
                        n = t - 2
                        for i, (t0, t1) in enumerate(LOADS):
                            if n % NSB == t0:
                                dve.wait_ge(slots_in[n // NSB][i], 16)
                                dve.tensor_copy(token[:, n:n + t1 - t0], XS[:, n:n + t1 - t0, R_ID])
                        dve.wait_ge(y_full, n + 1)
                        link(dve.tensor_tensor(YB[:, n % 2], acc[n % 2][:, 0:D], B2[:, bass.ds(expert[n] * D, D)], ALU.add))
                        dve.scalar_tensor_tensor(XS[:, n, 0:D], YB[:, n % 2], XS[:, n, R_P:R_P + 1], XS[:, n, 0:D],
                                                 ALU.mult, ALU.add).then_inc(z_ready, 1)

        @block.tensor
        def _(pe):
            def wait_reader(key):
                by = reader(key)
                for signal, value in by if isinstance(by, list) else [by]:
                    pe.wait_ge(signal, value)

            def hold(key):
                if key in before:
                    wait_reader(before[key])

            expert = {}
            for s in steps:
                kind = s[0]
                if kind == "xt":
                    _, st, b = s
                    if nth[s] == 0:
                        pe.wait_ge(in_con, 16)
                    hold(s)
                    pe.wait_ge(xn_ready, NQ * (nth["ln", st, b] + 1))
                    for t in range(NQ):
                        xn = ROW[:, b * NQ + t, D:2 * D] if st == 3 else XN[:, b, t]
                        ins = pe.transpose(bank(s)[:, 128 * t:128 * t + 128], xn, ident)
                    ins.then_inc(full[use[s][0]], 1)
                elif kind == "kp":
                    l = s[1]
                    pe.wait_ge(in_att[l], 32 if l == 0 else 16)
                    pe.wait_ge(in_ctx, 16)
                    for g in range(G):
                        key = (*s, g // 2)
                        if g % 2 == 0:
                            hold(key)
                        ins = pe.matmul(bank(key)[0:QR, (g % 2) * B * KEYS:(g % 2 + 1) * B * KEYS].rearrange("p (b k) -> p b k", b=B),
                                        ATT[l][:, A_K + QR * g:A_K + QR * (g + 1)], CTX[:, :, 0:KEYS], start=True, stop=True)
                        if g % 2 == 1:
                            ins.then_inc(full[use[key][0]], 1)
                elif kind == "vp":
                    _, l, b, j = s
                    if (b, j) == (0, 0):
                        pe.wait_ge(in_att[l], 32 if l == 0 else 16)
                        pe.wait_ge(in_ctx, 16)
                    hold(s)
                    w, k0 = WIDTHS[j], STARTS[j] % KEYS
                    pe.matmul(bank(s)[0:w, 0:D], CTX[:, b, k0:k0 + w], ATT[l][:, A_V:A_V + D],
                              start=True, stop=True).then_inc(full[use[s][0]], 1)
                elif kind == "q":
                    _, l, b, g = s
                    pe.wait_ge(xnt_ready, nth["xt", 2 * l, b] + 1)
                    hold(s)
                    pe.matmul(bank(s)[0:QR, :], ATT[l][:, A_Q + QR * g:A_Q + QR * (g + 1)], XNT[:, b], start=True,
                              stop=True).then_inc(full[use[s][0]], 1)
                elif kind == "max":
                    _, l, b, i = s
                    n = nth[s]
                    g, qt = divmod(i, NQ)
                    if qt == 0:
                        pe.wait_ge(ql_ready, nth["q", l, b, g] + 1)
                        if (l, b) == (0, 0):
                            pe.wait_ge(kg_dve, min(g, 1) + 1)
                        else:
                            pe.wait_ge(kg_pool, 2 * (2 * l + b - 1) + min(g, 1) + 1)
                    if i == 0:
                        pe.wait_ge(zeroed, (4, 7)[b])
                    hold(s)
                    off = PAD * (g % 2)
                    pe.matmul(bank(s)[:, 0:GK], QG[0:ONES + 2, b, g, 128 * qt:128 * qt + 128],
                              KG[0:ONES + 2, b, g, off:off + GK], start=True, stop=True).then_inc(full[use[s][0]], 1)
                elif kind == "mt":
                    _, l, b, half = s
                    hold(s)
                    pe.wait_ge(max_read, nth["max", l, b, 2 * NQ * (half + 1) - 1] + 1)
                    pe.wait_ge(zeroed, 6)
                    for t in range(NQ):
                        m = MR[:, b, t, 2 * half:2 * half + 2].rearrange("p g c -> p (g c)")
                        ins = pe.transpose(bank(s)[0:64, 128 * t:128 * t + 128], m, ident)
                    ins.then_inc(full[use[s][0]], 1)
                elif kind == "sc":
                    _, l, b, t = s
                    n = nth[s]
                    half, j = divmod(t, NT)
                    w = WIDTHS[j]
                    if j == 0:
                        pe.wait_ge(m_act, nth["mt", l, b, half] + 1)
                        pe.wait_ge(m_dve, nth["mt", l, b, half] + 1)
                    if n >= 2:
                        pe.wait_ge(probs_ready, n - 1)
                    parts = {0: [(0, 0)], 1: [(0, 123)], 2: [(0, 246), (1, 0)], 3: [(1, 124)], 4: [(1, 247)]}[j]
                    for i, (odd, c) in enumerate(parts):
                        g = 2 * half + odd
                        ins = pe.matmul(scores[n % 2][0:w, :], KG[:, b, g, c:c + w], QG[:, b, g],
                                        start=(i == 0), stop=(i == len(parts) - 1))
                    ins.then_inc(scores_ready, 1)
                elif kind == "pv":
                    _, l, b, t = s
                    n = nth[s]
                    half, j = divmod(t, NT)
                    w = WIDTHS[j]
                    if t == 0:
                        pe.wait_ge(v_ready, NT * (B * l + b + 1))
                        pe.wait_ge(zeroed, 8)
                        pe.wait_ge(ones_col, 2 * (B * l + b + 1))
                        if n > 0:
                            pe.wait_ge(on_ready, 2 * nth["on", l, b])
                    pe.wait_ge(probs_ready, n + 1)
                    cols = HALF * VC
                    for qt in range(NQ):
                        c = (qt % 2) * 2 * cols + half * cols
                        ins = pe.matmul(acc[qt // 2][:, c:c + VW], P[0:w, n % NP, 128 * qt:128 * qt + 128],
                                        VP[0:w, l, b, j, half],
                                        start=(t == 0 and qt % 2 == 0), stop=(t == 2 * NT - 1 and qt % 2 == 1),
                                        skip_group_check=True)
                    ins.then_inc(probs_used, 1)
                elif kind == "ot":
                    _, l, b = s
                    hold(s)
                    pe.wait_ge(on_ready, 2 * (nth["on", l, b] + 1))
                    for t in range(NQ):
                        ins = pe.transpose(bank(s)[:, 128 * t:128 * t + 128], ON[:, b, t], ident)
                    ins.then_inc(full[use[s][0]], 1)
                elif kind == "wo":
                    _, l, b = s
                    hold(s)
                    pe.wait_ge(ot_ready, nth["ot", l, b] + 1)
                    for t in range(NQ):
                        ins = pe.matmul(bank(s)[:, D * t:D * (t + 1)], OT[:, b, 128 * t:128 * t + 128],
                                        ATT[l][:, A_O:A_O + D], start=True, stop=True)
                    ins.then_inc(full[use[s][0]], 1)
                elif kind in ("gate", "route"):
                    b = s[1]
                    st = 1 if kind == "gate" else 3
                    width = E + E * R if kind == "gate" else E
                    w = W0[:, W_GA:W_GA + width] if kind == "gate" else SW[:, :]
                    if b == 0:
                        pe.wait_ge(*((in_w0, 16) if kind == "gate" else (in_moe, 48)))
                    hold(s)
                    pe.wait_ge(xnt_ready, nth["xt", st, b] + 1)
                    for t in range(NQ):
                        ins = pe.matmul(bank(s)[:, width * t:width * (t + 1)], XNT[:, b, 128 * t:128 * t + 128], w,
                                        start=True, stop=True)
                    ins.then_inc(full[use[s][0]], 1)
                elif kind == "ut":
                    b = s[1]
                    hold(s)
                    pe.wait_ge(u3_ready, 3 * (nth[s] + 1))
                    for t in range(NQ):
                        ins = pe.transpose(bank(s)[0:QR, 128 * t:128 * t + 128], U3[:, b, t], ident)
                    ins.then_inc(full[use[s][0]], 1)
                elif kind == "hid":
                    _, b, k = s
                    hold(s)
                    pe.matmul(bank(s)[:, :], W0[:, W_WI + 128 * k:W_WI + 128 * (k + 1)], XNT[:, b], start=True, stop=False)
                    if k == 0:
                        pe.wait_ge(u_ready, nth["ut", b] + 1)
                        pe.wait_ge(lb_ready, 1)
                    pe.matmul(bank(s)[:, :], LS[:, 128 * k:128 * (k + 1)], U[:, b], start=False,
                              stop=True).then_inc(full[use[s][0]], 1)
                elif kind == "out":
                    b = s[-1]
                    hold(s)
                    pe.wait_ge(hid_act, 2 * (b + 1))
                    pe.wait_ge(hid_dve, 2 * (b + 1))
                    for t in range(NQ):
                        for k in range(NF):
                            w = W0[:, W_WO + D * k:W_WO + D * (k + 1)]
                            ins = pe.matmul(bank(s)[:, D * t:D * (t + 1)], HT[:, b, k, 128 * t:128 * t + 128], w,
                                            start=(k == 0), stop=(k == NF - 1))
                    ins.then_inc(full[use[s][0]], 1)
                elif kind == "rank":
                    b = s[1]
                    hold(s)
                    pe.wait_ge(hot_ready, b + 1)
                    pe.wait_ge(binary, 2)
                    ps = bank(s)
                    pe.matmul(ps[:, 0:NQ * E], trib[:, :], hotb[:, b * NQ:(b + 1) * NQ, :].rearrange("p t e -> p (t e)"),
                              start=True, stop=False, skip_group_check=True)
                    for i in range(NQ):
                        n = NQ - i
                        ins = pe.matmul(ps[:, E * (i + 1):E * (NQ + 1)].rearrange("p (t e) -> p t e", e=E), onesb[:, :],
                                        hotb[:, b * NQ + i].unsqueeze(1).to_broadcast([128, n, E]), start=False, stop=(i == NQ - 1),
                                        skip_group_check=True)
                    ins.then_inc(full[use[s][0]], 1)
                elif kind == "moe":
                    t = s[1]
                    if t == -1:
                        for e in range(E):
                            pe.wait_ge(in_w2[e], 16)
                        for i in (2, 3):
                            wait_reader([k for k in use if use[k][0] == i][-1])
                        pe.wait_ge(probs_ready, 2 * B * 2 * NT)
                    if t + 1 < NS:
                        n = t + 1
                        pe.wait_ge(tile_ready, n // NSB + 1)
                        expert[n] = pe.value_load(tile_e[0:1, n:n + 1], min_val=0, max_val=E - 1)
                        for i, (t0, t1) in enumerate(LOADS):
                            if n % NSB == t0:
                                pe.wait_ge(slots_in[n // NSB][i], 16)
                        if n >= 2:
                            pe.wait_ge(xst_ready, n - 1)
                        pe.transpose(xst_ps(n), XS[:, n, D:2 * D], ident).then_inc(xst_full, 1)
                    if 0 <= t < NS:
                        pe.wait_ge(xst_ready, t + 1)
                        pe.wait_ge(w1_ready, t + 1)
                        if t >= 2:
                            pe.wait_ge(biased, t - 1)
                        for k in range(NF):
                            ins = pe.matmul(hidden[t % 2][:, 128 * k:128 * (k + 1)], W1C[:, t % 2, 128 * k:128 * (k + 1)],
                                            XST[:, t % 2], start=True, stop=True)
                        ins.then_inc(hidden_full, 1)
                    if t >= 2:
                        n = t - 2
                        pe.wait_ge(gelu_ready, n + 1)
                        if n == 0:
                            pe.wait_ge(on_ready, 2 * 2 * B)
                        if n >= 2:
                            pe.wait_ge(z_ready, n - 1)
                        for k in range(NF):
                            ins = pe.matmul(acc[n % 2][:, 0:D], HG1[:, n % NHB, 128 * k:128 * (k + 1)],
                                            W2[:, bass.ds(expert[n] * (NF * D) + D * k, D)], start=(k == 0), stop=(k == NF - 1))
                        ins.then_inc(y_full, 1)


_INS = ["x", "ctx3", "att0", "att1", "consts", "rows", "delta", "tau", "ffn0w", "loraB", "sw", "w1", "b1", "w2", "b2"]


def constants():
    c = np.zeros((128, C_N), np.float32)
    c[:, C_ID:C_ID + 128] = np.eye(128)
    for j in range(NT):
        for r in range(WIDTHS[j]):
            c[r, C_VM + HALF * j + (STARTS[j] + r) // KEYS] = 1
    for r in range(QR):
        c[r, C_KM + (r % 32) // DK] = 1
    c[ONES:ONES + 2, C_KM:C_KM + HG] = 1
    c[:, C_EW:C_EW + E] = np.arange(E, 0, -1)
    c[ONES, C_SEL] = 1
    c[ONES + 1, C_SEL + 1] = 1
    for h in range(HG):
        c[ONES + 2 + h, C_KM + h] = 1
        c[ONES + 2 + h, C_SEL + 2] = 1
    p = np.arange(128)
    for t in range(TILES):
        c[:, C_TAIL + 4 * t + 1] = 128 * t + p
    for t in range(NS):
        c[:, C_SID + t] = B * S + 128 * t + p
    c[:, C_T:C_T + NSB] = np.arange(NSB)
    c[:, C_THR:C_THR + NQ] = 128 * np.arange(NQ)
    c[:, C_LOW:C_LOW + E * E] = np.tri(E, E, -1).reshape(-1)
    c[:, C_TRI:C_TRI + 128] = np.tri(128, 128, -1).T
    return c


def kernel(**inputs):
    import concourse.bacc as _bacc
    from concourse.bass_utils import run_bass_kernel_spmd as _run

    a = {k: np.asarray(v) for k, v in inputs.items()}

    def attention_weights(l):
        p = f"L{l}_xcond_"
        out = np.zeros((128, A_N), np.float32)
        for g in range(G):
            for i in range(3):
                rows_ = slice(32 * g, 32 * g + 32)
                for c, cb, n in ((A_K, A_BK, "k"), (A_Q, A_BQ, "q")):
                    out[:, c + QR * g + 32 * i:c + QR * g + 32 * (i + 1)] = a[p + "W" + n][rows_].T
                    out[32 * i:32 * (i + 1), cb + g] = a[p + "b" + n][rows_]
        out[:, A_V:A_V + D] = a[p + "Wv"].T
        out[:, A_O:A_O + D] = a[p + "Wo"].T
        out[:, A_BV] = a[p + "bv"]
        return out

    ctx_t = a["ctx_1024"].transpose(2, 0, 1)
    f0 = "L0_ffn_"
    by_tile = lambda w: w.reshape(NF, 128, -1).transpose(1, 0, 2).reshape(128, -1)
    arrays = {
        "x": a["x"].reshape(B * S, D),
        "ctx3": np.concatenate([ctx_t] * 3, axis=2),
        "att0": attention_weights(0),
        "att1": attention_weights(1),
        "consts": constants(),
        "rows": np.concatenate([a["L0_xcond_bo"], a[f0 + "wo_b"], a["L1_xcond_bo"], a[f0 + "gate_b"], a["L1_ffn_switch_b"]]),
        "delta": a["fside_BxS2_0"].reshape(-1),
        "tau": a["condB_tau"],
        "ffn0w": np.concatenate([a[f0 + "gate_W"].T, a[f0 + "lora_A"].reshape(E * R, D).T, a[f0 + "wi_W"].T,
                                 by_tile(a[f0 + "wo_W"].T), a[f0 + "wi_b"].reshape(NF, 128).T], axis=1),
        "loraB": a[f0 + "lora_B"].transpose(0, 2, 1).reshape(E * R, F),
        "sw": a["L1_ffn_switch_w"],
        "w1": a["L1_ffn_w1"].transpose(1, 0, 2),
        "b1": a["L1_ffn_b1"].reshape(E, NF, 128).transpose(2, 0, 1).reshape(128, E * NF),
        "w2": a["L1_ffn_w2"].reshape(E, NF, 128, D).transpose(2, 0, 1, 3).reshape(128, E, NF * D),
        "b2": a["L1_ffn_b2"].reshape(-1),
    }
    nc = _bacc.Bacc("TRN2", target_bir_lowering=False, num_devices=1)
    feeds, args = {}, []
    for name in _INS:
        v = np.ascontiguousarray(arrays[name])
        feeds[f"in_{name}"] = v
        args.append(nc.dram_tensor(f"in_{name}", v.shape, mybir.dt.from_np(v.dtype), kind="ExternalInput").ap())
    out = nc.dram_tensor("out", (B * S, D), F32, kind="ExternalOutput").ap()
    build(nc, *args, out)
    r = _run(nc, [feeds], core_ids=[0])
    return r.results[0]["out"].reshape(B, S, D)
```
